# Optimizing a Trainium2 kernel written in Bass

```python
import numpy as np
import jax
import jax.numpy as jnp

def _softmax(x, axis=-1):
    return jax.nn.softmax(x, axis=axis)

def _gelu(x):
    return jax.nn.gelu(x, approximate=True)

def _silu(x):
    return jax.nn.silu(x)

def _sigmoid(x):
    return jax.nn.sigmoid(x)

def _layernorm(x, axis=-1, eps=1e-05):
    m = jnp.mean(x, axis=axis, keepdims=True)
    v = jnp.var(x, axis=axis, keepdims=True)
    return (x - m) / jnp.sqrt(v + eps)

def _scatter_add(tgt, idx, src, axis=0):
    return tgt.at[idx].add(src)

def _segment_sum(src, seg, n):
    return jax.ops.segment_sum(src, seg, n)
kernel_name = 'mk_recurrent_d1_jaxref_r4_51abd4'

def setup_inputs(seed: int=0):
    np.random.seed(seed)
    _w = jnp.asarray

    def _L0_attn_setup():
        import jax, jax.numpy as jnp
        import numpy as np
        H, HKV, HD = (16, 4, 128)

        def _rope(x, cos, sin):
            xr = x.reshape(*x.shape[:-1], HD // 2, 2)
            a, b = (xr[..., 0], xr[..., 1])
            c = cos[None, :, None, :]
            s = sin[None, :, None, :]
            return jnp.stack([a * c - b * s, a * s + b * c], axis=-1).reshape(x.shape)
        key = jax.random.key(seed)
        ks = jax.random.split(key, 5)
        B, T, C = (2, 512, 512)
        std = 0.02
        return {'x': jax.random.normal(ks[0], (B, T, C), jnp.float32), 'Wq': jax.random.normal(ks[1], (C, H * HD), jnp.float32) * std, 'bq': jnp.zeros((H * HD,), jnp.float32), 'Wk': jax.random.normal(ks[2], (C, HKV * HD), jnp.float32) * std, 'bk': jnp.zeros((HKV * HD,), jnp.float32), 'Wv': jax.random.normal(ks[3], (C, HKV * HD), jnp.float32) * std, 'bv': jnp.zeros((HKV * HD,), jnp.float32), 'Wo': jax.random.normal(ks[4], (H * HD, C), jnp.float32) * std, 'bo': jnp.zeros((C,), jnp.float32)}
    _L0_attn_in = _L0_attn_setup()

    def _L0_ffn_setup():
        import jax, jax.numpy as jnp
        import numpy as np
        E = 32
        K = 6
        H = 512
        I = 256
        T = 512
        CAP = 192
        SCALE = 1.5
        SWIGLU_LIMIT = 10.0
        key = jax.random.key(seed)
        ks = jax.random.split(key, 9)

        def s(k, shape, fan):
            return jax.random.normal(k, shape, jnp.float32) * fan ** (-0.5)
        return {'x': jax.random.normal(ks[0], (1, T, H), jnp.float32), 'gate_w': s(ks[1], (E, H), H), 'bias': jax.random.normal(ks[2], (E,), jnp.float32) * 0.01, 'w_gate': s(ks[3], (E, I, H), H), 'w_up': s(ks[4], (E, I, H), H), 'w_down': s(ks[5], (E, H, I), I), 'sg': s(ks[6], (I, H), H), 'su': s(ks[7], (I, H), H), 'sd': s(ks[8], (H, I), I)}
    _L0_ffn_in = _L0_ffn_setup()
    _d = {'L0_attn_x': _L0_attn_in['x'], 'L0_attn_Wq': _L0_attn_in['Wq'], 'L0_attn_bq': _L0_attn_in['bq'], 'L0_attn_Wk': _L0_attn_in['Wk'], 'L0_attn_bk': _L0_attn_in['bk'], 'L0_attn_Wv': _L0_attn_in['Wv'], 'L0_attn_bv': _L0_attn_in['bv'], 'L0_attn_Wo': _L0_attn_in['Wo'], 'L0_attn_bo': _L0_attn_in['bo'], 'L0_ffn_gate_w': _L0_ffn_in['gate_w'], 'L0_ffn_bias': _L0_ffn_in['bias'], 'L0_ffn_w_gate': _L0_ffn_in['w_gate'], 'L0_ffn_w_up': _L0_ffn_in['w_up'], 'L0_ffn_w_down': _L0_ffn_in['w_down'], 'L0_ffn_sg': _L0_ffn_in['sg'], 'L0_ffn_su': _L0_ffn_in['su'], 'L0_ffn_sd': _L0_ffn_in['sd']}
    _x0 = _d['L0_attn_x']
    _d['L0_attn_x'] = jax.random.normal(jax.random.fold_in(jax.random.key(seed), 1), (1, 2048, 512), dtype=_x0.dtype)
    del _x0
    return _d

def reference(L0_attn_x, L0_attn_Wq, L0_attn_bq, L0_attn_Wk, L0_attn_bk, L0_attn_Wv, L0_attn_bv, L0_attn_Wo, L0_attn_bo, L0_ffn_gate_w, L0_ffn_bias, L0_ffn_w_gate, L0_ffn_w_up, L0_ffn_w_down, L0_ffn_sg, L0_ffn_su, L0_ffn_sd):

    def _L0_attn_ref(x, Wq, bq, Wk, bk, Wv, bv, Wo, bo):
        import jax, jax.numpy as jnp
        import numpy as np
        H, HKV, HD = (16, 4, 128)

        def _rope(x, cos, sin):
            xr = x.reshape(*x.shape[:-1], HD // 2, 2)
            a, b = (xr[..., 0], xr[..., 1])
            c = cos[None, :, None, :]
            s = sin[None, :, None, :]
            return jnp.stack([a * c - b * s, a * s + b * c], axis=-1).reshape(x.shape)
        B, T, C = x.shape
        G = H // HKV
        q = (x @ Wq + bq).reshape(B, T, H, HD)
        k = (x @ Wk + bk).reshape(B, T, HKV, HD)
        v = (x @ Wv + bv).reshape(B, T, HKV, HD)
        theta = 1.0 / 10000.0 ** (jnp.arange(0, HD, 2, dtype=jnp.float32) / HD)
        freqs = jnp.arange(T, dtype=jnp.float32)[:, None] * theta[None, :]
        cos, sin = (jnp.cos(freqs), jnp.sin(freqs))
        q = _rope(q, cos, sin)
        k = _rope(k, cos, sin)
        q = q.transpose(0, 2, 1, 3).reshape(B, G, HKV, T, HD)
        k = k.transpose(0, 2, 1, 3)
        v = v.transpose(0, 2, 1, 3)
        scale = 1.0 / np.sqrt(H).astype(np.float32)
        scores = jnp.einsum('bgjtd,bjsd->bgjts', q, k) * scale
        mask = jnp.tril(jnp.ones((T, T), dtype=bool))
        scores = jnp.where(mask[None, None, None], scores, -jnp.inf)
        wei = jax.nn.softmax(scores, axis=-1)
        out = jnp.einsum('bgjts,bjsd->bgjtd', wei, v)
        out = out.transpose(0, 3, 1, 2, 4).reshape(B, T, H * HD)
        return out @ Wo + bo

    def _L0_ffn_ref(x, gate_w, bias, w_gate, w_up, w_down, sg, su, sd):
        import jax, jax.numpy as jnp
        import numpy as np
        E = 32
        K = 6
        H = 512
        I = 256
        T = 512
        CAP = 192
        SCALE = 1.5
        SWIGLU_LIMIT = 10.0
        B, S, Hd = x.shape
        h = x.reshape(-1, Hd)
        logits = h @ gate_w.T
        scores = jnp.sqrt(jax.nn.softplus(logits))
        _, topk_idx = jax.lax.top_k(scores + bias[None, :], K)
        topk_w = jnp.take_along_axis(scores, topk_idx, axis=1)
        topk_w = topk_w / jnp.sum(topk_w, axis=-1, keepdims=True)
        topk_w = topk_w * SCALE
        eid = topk_idx.reshape(-1)
        onehot = jax.nn.one_hot(eid, E, dtype=jnp.int32)
        pos = jnp.cumsum(onehot, axis=0) - 1
        pos = jnp.take_along_axis(pos, eid[:, None], axis=1)[:, 0]
        valid = pos < CAP
        pos = jnp.where(valid, pos, CAP)
        h_rep = jnp.repeat(h, K, axis=0)
        xb = jnp.zeros((E, CAP + 1, Hd), x.dtype).at[eid, pos].set(h_rep)
        g = jnp.einsum('ech,eih->eci', xb, w_gate)
        u = jnp.einsum('ech,eih->eci', xb, w_up)
        inter = jax.nn.silu(g) * u
        yb = jnp.einsum('eci,ehi->ech', inter, w_down)
        w_slot = jnp.where(valid, topk_w.reshape(-1), 0.0)
        y = yb[eid, pos] * w_slot[:, None]
        routed = y.reshape(-1, K, Hd).sum(axis=1)
        si = jax.nn.silu(h @ sg.T) * (h @ su.T)
        si = jnp.clip(si, -SWIGLU_LIMIT, SWIGLU_LIMIT)
        shared = si @ sd.T
        return (routed + shared).reshape(B, S, Hd)
    x = L0_attn_x
    xn = _layernorm(x, axis=-1)
    s = _L0_attn_ref(xn, L0_attn_Wq, L0_attn_bq, L0_attn_Wk, L0_attn_bk, L0_attn_Wv, L0_attn_bv, L0_attn_Wo, L0_attn_bo)
    g = _silu(_L0_ffn_ref(xn, L0_ffn_gate_w, L0_ffn_bias, L0_ffn_w_gate, L0_ffn_w_up, L0_ffn_w_down, L0_ffn_sg, L0_ffn_su, L0_ffn_sd))
    x = x + s * g
    return x

_drawn_inputs = setup_inputs


def setup_inputs(seed=0):
    import zlib

    import numpy as np

    out = dict(_drawn_inputs(seed))
    spreads = {'L0_attn_bq': (0.0, 0.8),
     'L0_attn_bk': (0.0, 0.8),
     'L0_attn_bv': (0.0, 0.1),
     'L0_attn_bo': (0.0, 0.1)}
    factors = {'L0_attn_Wq': 8.0,
     'L0_attn_Wk': 8.0,
     'L0_attn_Wv': 4.703,
     'L0_ffn_gate_w': 3.037,
     'L0_ffn_bias': 8.0,
     'L0_ffn_w_gate': 2.903,
     'L0_ffn_w_up': 2.718,
     'L0_ffn_w_down': 2.733}
    for name, (base, spread) in spreads.items():
        noise = np.random.default_rng([zlib.crc32(name.encode()), seed]).standard_normal(out[name].shape)
        drawn = base * np.exp(spread * noise) if base else spread * noise
        out[name] = jnp.asarray(drawn.astype(out[name].dtype))
    for name, factor in factors.items():
        out[name] = (out[name] * factor).astype(out[name].dtype)
    return out
```

```python
from contextlib import ExitStack

import numpy as np

import concourse.bass as bass
from concourse import mybir

F32 = mybir.dt.float32
F32R = mybir.dt.float32r
BF16 = mybir.dt.bfloat16
U32 = mybir.dt.uint32
ACT = mybir.ActivationFunctionType
ALU = mybir.AluOpType
AX = mybir.AxisListType

P = 128
T, C = 2048, 512
HEADS, KV, HD = 16, 4, 128
G = HEADS // KV
E, K, CAP = 32, 6, 192
I = 256
NT, NC = T // P, C // P
TG, NG = 512, T // 512
NI = I // P
HALF = CAP // 2
ROUTE_SCALE = 1.5
CLIP = 10.0
EPS = 1e-5
FAR = float(1 << 20)
QSCALE = HEADS ** -0.5
ROPED = HEADS + KV

C_ID, C_MASK, C_UPPER, C_ONES, C_ITEM, C_BASE = 0, 128, 256, 384, 512, 544
C_END = 576


def constant_table():
    t = np.zeros((P, C_END), np.float32)
    t[:, C_ID:C_ID + P] = np.eye(P)
    t[:, C_MASK:C_MASK + P] = np.triu(np.full((P, P), -1e30), 1)
    t[:, C_UPPER:C_UPPER + P] = np.triu(np.ones((P, P)), 1)
    t[:, C_ONES:C_ONES + P] = 1.0
    t[:, C_ITEM:C_ITEM + E] = np.arange(E)
    t[:, C_BASE:C_BASE + E] = np.arange(E) * CAP
    return t


def rope_table():
    half = np.arange(0, HD, 2, dtype=np.float32) / np.float32(HD)
    theta = np.float32(1.0) / (np.float64(10000.0) ** half).astype(np.float32)
    freq = (theta[:, None] * np.arange(T, dtype=np.float32)[None, :]).astype(np.float64)
    cos, sin = np.cos(freq).astype(np.float32), np.sin(freq).astype(np.float32)
    return np.stack([np.concatenate([cos, cos]), np.concatenate([-sin, sin])], axis=1).copy()


def three_passes(nc, out, a_hi, a_lo, b_hi, b_lo, first, last):
    nc.tensor.matmul(out, a_hi, b_hi, start=first, stop=False)
    nc.tensor.matmul(out, a_hi, b_lo, start=False, stop=False)
    return nc.tensor.matmul(out, a_lo, b_hi, start=False, stop=last)


def project(nc, ins, d, keep):
    with ExitStack() as ctx:
        sb = lambda n, s, dt=F32: ctx.enter_context(nc.sbuf_tensor(n, s, dt))
        sem = lambda n: ctx.enter_context(nc.semaphore(n))
        xn = sb("xn", [P, NT, C])
        xt_hi, xt_lo = sb("xt_hi", [P, NC, T], F32R), sb("xt_lo", [P, NC, T], F32R)
        wv = sb("wv", [P, NC, C])
        wv_hi, wv_lo = sb("wv_hi", [P, NC, C], F32R), sb("wv_lo", [P, NC, C], F32R)
        bv = sb("bv_row", [1, C])
        bv_hi, bv_lo = sb("bv_hi", [1, C], F32R), sb("bv_lo", [1, C], F32R)
        one_r = sb("one_r", [1, P], F32R)
        gw = sb("gw", [P, NC, E])
        gw_hi, gw_lo = sb("gw_hi", [P, NC, E], F32R), sb("gw_lo", [P, NC, E], F32R)
        ebias = sb("ebias", [P, E])
        rope = sb("rope", [P, 2, T])
        stats, mv = sb("stats", [P, NT, 6]), sb("mv", [P, NT, 2])
        var, sd, rstd, tmp = (sb(n, [P, NT]) for n in ("var", "sd", "rstd", "tmp"))
        w_raw = sb("w_raw", [P, 2, C + 1])
        w_hi, w_lo = sb("w_hi", [P, 2, C], F32R), sb("w_lo", [P, 2, C], F32R)
        swapped = sb("swapped", [P, 2, TG])
        t1, t2 = sb("t1", [P, NG, TG]), sb("t2", [P, NG, TG])
        row_out = sb("row_out", [P, 4, C])
        inter_lo = sb("inter_lo", [P, NI, TG], F32R)
        zero_u = sb("zero_u", [P, E * CAP // P], U32)
        sel_b, before_b = sb("sel_b", [P, NT, E], BF16), sb("before_b", [P, NT, E], BF16)
        ones_b, upper_b = sb("ones_b", [P, P], BF16), sb("upper_b", [P, P], BF16)
        top = sb("top", [P, NT, 8])
        topi = sb("topi", [P, NT, 8], U32)
        topf = sb("topf", [P, NT, 8])
        wk, dk = sb("wk", [P, K, NT]), sb("dk", [P, K, NT])
        wsum, wrec = sb("wsum", [P, NT]), sb("wrec", [P, NT])
        scat = sb("scat", [P, K, NT], U32)
        tok = sb("tok", [P, NT], U32)
        cst = keep["cst"]
        sgu, sdn = xn[:, 0:4, :], xn[:, 4:6, :]
        route = lambda k: xn[:, 6 + k, :].rearrange("p (n e) -> p n e", e=E)
        hot = lambda k: route(k)
        logit, ra, rb, rc = (route(6 + k) for k in range(4))
        sgu_hi, sgu_lo = wv_hi, wv_lo
        sdn_hi, sdn_lo = w_hi, w_lo
        inter_hi = sb("inter_hi", [P, NI, TG], F32R)

        p_t = ctx.enter_context(nc.psum_tensor("p_t", [P, 2, 512], F32))
        p_p = ctx.enter_context(nc.psum_tensor("p_p", [P, 4, 512], F32))
        p_v = ctx.enter_context(nc.psum_tensor("p_v", [P, 2, 512], F32))
        ident = cst[:, C_ID:C_ID + P]
        p_logit = p_p[:, 2, :].rearrange("p (n e) -> p n e", e=E)
        p_pos = p_t[:, 0, :].rearrange("p (n e) -> p n e", e=E)

        x_loaded = [sem(f"x_loaded{q}") for q in range(NG)]
        const_loaded, wv_loaded, rope_loaded, tok_loaded = (
            sem(n) for n in ("const_loaded", "wv_loaded", "rope_loaded", "tok_loaded"))
        var_ready, sd_ready, xn_ready, xn_stored = (sem(n) for n in ("var_ready", "sd_ready", "xn_ready", "xn_stored"))
        chain = sem("chain")
        wv_hi_ready, wv_ready = sem("wv_hi_ready"), sem("wv_ready")
        xt_psum, xt_hi_ready, xt_ready = sem("xt_psum"), sem("xt_hi_ready"), sem("xt_ready")
        logits_ready, v_psum, v_evicted = sem("logits_ready"), sem("v_psum"), sem("v_evicted")
        row_stored = [sem(f"row_stored{k}") for k in range(4)]
        na_ready, exp_ready, lnin_ready, ln_ready, sp_ready, sqrt_ready = (
            sem(n) for n in ("na_ready", "exp_ready", "lnin_ready", "ln_ready", "sp_ready", "sqrt_ready"))
        sel_ready, pos_ready, route_ready = sem("sel_ready"), sem("pos_ready"), sem("route_ready")
        zero_ready, table_cleared, scattered = sem("zero_ready"), sem("table_cleared"), sem("scattered")
        w_loaded = [sem(f"w_loaded{b}") for b in range(2)]
        w_hi_ready, w_ready = sem("w_hi_ready"), sem("w_ready")
        qk_psum, swap_ready, t2_done, rot_ready = sem("qk_psum"), sem("swap_ready"), sem("t2_done"), sem("rot_ready")
        rot_stored = [sem(f"rot_stored{u}") for u in range(NG)]
        shared_loaded, shared_hi_ready, shared_ready = (
            sem("shared_loaded"), sem("shared_hi_ready"), sem("shared_ready"))
        gu_psum, silu_ready, gu_read, inter_ready = sem("gu_psum"), sem("silu_ready"), sem("gu_read"), sem("inter_ready")
        down_psum, down_evicted = sem("down_psum"), sem("down_evicted")
        block = ctx.enter_context(nc.Block())
        PAIRS = ROPED // 2
        xv = ins["x"].rearrange("(n p) c -> p n c", p=P)
        xnv = d["xn"].rearrange("(n p) c -> p n c", p=P)

        @block.sync
        def _(sp):
            for q in range(NG):
                sp.dma_start(xn[:, 4 * q:4 * q + 4, :], xv[:, 4 * q:4 * q + 4, :]).then_inc(x_loaded[q], 16)
            sp.dma_start(rope[:, :, :], ins["rope"]).then_inc(rope_loaded, 16)
            for b in range(2):
                sp.dma_start(w_raw[:, b, :], ins["wqk"][b]).then_inc(w_loaded[b], 16)
            for q in range(NG):
                sp.wait_ge(xn_ready, 4 * q + 4)
                sp.dma_start(xnv[:, 4 * q:4 * q + 4, :], xn[:, 4 * q:4 * q + 4, :]).then_inc(xn_stored, 16)
            sp.wait_ge(zero_ready, 1)
            sp.dma_start(d["slot_token"].rearrange("(p n) o -> p (n o)", p=P), zero_u[:, :]).then_inc(table_cleared, 16)
            for t in range(NT):
                sp.wait_ge(v_evicted, t + 1)
                sp.dma_start(d["v"][t * P:(t + 1) * P, :], row_out[:, t % 4, :]).then_inc(row_stored[t % 4], 16)
            sp.wait_ge(xn_stored, 16 * NG)
            sp.wait_ge(xt_psum, NT)
            sp.dma_start(sgu, ins["sgu"]).then_inc(shared_loaded, 16)
            sp.dma_start(sdn, ins["sdn"]).then_inc(shared_loaded, 16)
            for u in range(NG):
                sp.sem_inc(rot_stored[u], 16)

            def store(n):
                for u in range(NG):
                    sp.wait_ge(rot_ready, 4 * n + u + 1)
                    sp.dma_start(d["qk"][bass.ds(n, 1), :, u * TG:(u + 1) * TG], t1[:, u:u + 1, :])\
                      .then_inc(rot_stored[u], 16)
            with sp.Fori(0, PAIRS - 1) as i:
                for b in range(2):
                    store(2 * i + b)
                    sp.dma_start(w_raw[:, b:b + 1, :], ins["wqk"][bass.ds(2 * i + b + 2, 1)].rearrange("a p c -> p a c"))\
                      .then_inc(w_loaded[b], 16)
            store(ROPED - 2)
            store(ROPED - 1)
            for u in range(NG):
                sp.wait_ge(rot_stored[u], 16 * (ROPED + 1))
            for t in range(NT):
                sp.wait_ge(down_evicted, t + 1)
                sp.dma_start(d["shared"][t * P:(t + 1) * P, :], row_out[:, t % 4, :]).then_inc(row_stored[t % 4], 16)
            for k in range(4):
                sp.wait_ge(row_stored[k], 16 * 8)

        @block.gpsimd
        def _(pool):
            pool.memset(zero_u[:, :], 0).then_inc(zero_ready, 1)
            pool.wait_ge(tok_loaded, 16)
            pool.wait_ge(table_cleared, 16)
            pool.wait_ge(route_ready, 1)
            for t in range(NT):
                for k in range(K):
                    pool.indirect_dma_start(
                        d["slot_token"], bass.IndirectOffsetOnAxis(ap=scat[:, k, t:t + 1], axis=0),
                        tok[:, t:t + 1], None, bounds_check=E * CAP - 1, oob_is_err=False).then_inc(scattered, 16)
            pool.wait_ge(scattered, 16 * NT * K)

        @block.scalar
        def _(act):
            act.dma_start(cst[:, :], ins["cst"]).then_inc(const_loaded, 16)
            act.dma_start(gw[:, :, :], ins["gate_w"]).then_inc(const_loaded, 16)
            act.dma_start(bv[:, :], ins["bv"]).then_inc(const_loaded, 16)
            act.dma_start(ebias[:, :], ins["ebias"].partition_broadcast(P)).then_inc(const_loaded, 16)
            act.dma_start(wv[:, :, :], ins["wv"]).then_inc(wv_loaded, 16)
            act.dma_start(tok[:, :], ins["tok"]).then_inc(tok_loaded, 16)
            for q in range(NG):
                act.wait_ge(var_ready, q + 1)
                nc.scalar.activation(sd[:, 4 * q:4 * q + 4], var[:, 4 * q:4 * q + 4], ACT.Sqrt).then_inc(sd_ready, 1)
                if q == 0:
                    act.wait_ge(wv_loaded, 16)
                    nc.scalar.activation(wv_hi[:, :, :], wv[:, :, :], ACT.Copy).then_inc(wv_hi_ready, 1)
            for t in range(NT):
                act.wait_ge(xt_psum, t + 1)
                nc.scalar.activation(xt_hi[:, :, t * P:(t + 1) * P],
                                     p_t[:, t % 2, :].rearrange("p (c n) -> p c n", c=NC), ACT.Copy).then_inc(xt_hi_ready, 1)
            def value_rows(t):
                act.wait_ge(v_psum, t + 1)
                if t >= 4:
                    act.wait_ge(row_stored[t % 4], 16 * (t // 4))
                nc.scalar.activation(row_out[:, t % 4, :], p_v[:, t % 2, :], ACT.Copy).then_inc(v_evicted, 1)
            value_rows(0)
            act.wait_ge(na_ready, 1)
            nc.scalar.activation(rb, ra, ACT.Exp).then_inc(exp_ready, 1)
            value_rows(1)
            act.wait_ge(lnin_ready, 1)
            nc.scalar.activation(hot(1), rc, ACT.Ln).then_inc(ln_ready, 1)
            value_rows(2)
            act.wait_ge(sp_ready, 1)
            nc.scalar.activation(ra, rb, ACT.Sqrt).then_inc(sqrt_ready, 1)
            for t in range(3, NT):
                value_rows(t)
            def weight_hi(b, count):
                act.wait_ge(w_loaded[b], 16 * count)
                nc.scalar.activation(w_hi[:, b, :], w_raw[:, b, 0:C], ACT.Copy).then_inc(w_hi_ready, 1)

            def head(n, b, count):
                for u in range(NG):
                    act.wait_ge(qk_psum, 4 * n + u + 1)
                    act.wait_ge(t2_done, 4 * n + u + 3)
                    h = HD // 2
                    nc.scalar.activation(swapped[0:h, u % 2, :], p_p[h:P, u, :], ACT.Identity, bias=w_raw[h:P, b, C:C + 1])
                    nc.scalar.activation(swapped[h:P, u % 2, :], p_p[0:h, u, :], ACT.Identity, bias=w_raw[0:h, b, C:C + 1])\
                      .then_inc(swap_ready, 1)
                    if u == 1 and count is not None:
                        weight_hi(1 - b, count)
            weight_hi(0, 1)
            with act.Fori(0, PAIRS - 1) as i:
                head(2 * i, 0, i + 1)
                head(2 * i + 1, 1, i + 2)
            head(ROPED - 2, 0, PAIRS)
            head(ROPED - 1, 1, None)
            act.wait_ge(shared_loaded, 32)
            act.wait_ge(v_psum, NT)
            for u in range(NI):
                act.wait_ge(rot_stored[u], 16 * (ROPED + 1))
            nc.scalar.activation(sgu_hi[:, :, :], sgu, ACT.Copy).then_inc(shared_hi_ready, 1)
            nc.scalar.activation(sdn_hi[:, :, :], sdn, ACT.Copy).then_inc(shared_hi_ready, 1)
            for g in range(NG):
                act.wait_ge(gu_psum, g + 1)
                for i in range(NI):
                    if g:
                        act.wait_ge(inter_ready, 2 * (g - 1) + i + 1)
                    nc.scalar.activation(t1[:, i, :], p_p[:, i, :], ACT.Silu).then_inc(silu_ready, 1)
                for r in range(4):
                    t = 4 * g + r
                    act.wait_ge(down_psum, t + 1)
                    act.wait_ge(row_stored[t % 4], 16 * (4 + t // 4))
                    nc.scalar.activation(row_out[:, t % 4, :], p_v[:, t % 2, :], ACT.Copy).then_inc(down_evicted, 1)

        @block.vector
        def _(dve):
            v = nc.vector
            steps = [0]

            def link(instruction):
                steps[0] += 1
                instruction.then_inc(chain, 1)
                dve.wait_ge(chain, steps[0])

            def publish(instruction, semaphore):
                instruction.then_inc(semaphore, 1)
                dve.wait_ge(semaphore, 1)

            dve.wait_ge(const_loaded, 64)
            v.tensor_copy(ones_b[:, :], cst[:, C_ONES:C_ONES + P])
            v.tensor_copy(upper_b[:, :], cst[:, C_UPPER:C_UPPER + P])
            v.tensor_copy(one_r[:, :], cst[0:1, C_ONES:C_ONES + P])
            v.tensor_copy(gw_hi[:, :, :], gw[:, :, :])
            link(v.tensor_copy(bv_hi[:, :], bv[:, :]))
            v.tensor_tensor(gw_lo[:, :, :], gw[:, :, :], gw_hi[:, :, :].bitcast(F32), ALU.subtract)
            v.tensor_tensor(bv_lo[:, :], bv[:, :], bv_hi[:, :].bitcast(F32), ALU.subtract)
            for q in range(NG):
                dve.wait_ge(x_loaded[q], 16)
                s = slice(4 * q, 4 * q + 4)
                for t in range(4 * q, 4 * q + 4):
                    last = v.bn_stats(stats[:, t, :], xn[:, t, :])
                link(last)
                for t in range(4 * q, 4 * q + 4):
                    last = v.bn_aggr(mv[:, t, :], stats[:, t, :])
                link(last)
                v.tensor_scalar(var[:, s], mv[:, s, 1], EPS, None, ALU.add).then_inc(var_ready, 1)
                dve.wait_ge(sd_ready, q + 1)
                link(v.reciprocal(rstd[:, s], sd[:, s]))
                link(v.tensor_tensor(tmp[:, s], rstd[:, s], rstd[:, s], ALU.mult))
                link(v.tensor_tensor(tmp[:, s], tmp[:, s], var[:, s], ALU.mult))
                link(v.tensor_scalar(tmp[:, s], tmp[:, s], -0.5, 1.5, ALU.mult, ALU.add))
                link(v.tensor_tensor(rstd[:, s], rstd[:, s], tmp[:, s], ALU.mult))
                for t in range(4 * q, 4 * q + 4):
                    v.tensor_scalar(xn[:, t, :], xn[:, t, :], mv[:, t, 0:1], rstd[:, t:t + 1],
                                    ALU.subtract, ALU.mult).then_inc(xn_ready, 1)
            dve.wait_ge(wv_hi_ready, 1)
            v.tensor_tensor(wv_lo[:, :, :], wv[:, :, :], wv_hi[:, :, :].bitcast(F32), ALU.subtract).then_inc(wv_ready, 1)
            for t in range(NT):
                dve.wait_ge(xt_hi_ready, t + 1)
                col = slice(t * P, (t + 1) * P)
                v.tensor_tensor(xt_lo[:, :, col], p_t[:, t % 2, :].rearrange("p (c n) -> p c n", c=NC),
                                xt_hi[:, :, col].bitcast(F32), ALU.subtract).then_inc(xt_ready, 1)
            dve.wait_ge(logits_ready, 1)
            dve.wait_ge(xn_stored, 16 * NG)
            link(v.tensor_copy(logit, p_logit))
            v.scalar_tensor_tensor(ra, logit, -1.0, logit, ALU.mult, ALU.min).then_inc(na_ready, 1)
            dve.wait_ge(exp_ready, 1)
            publish(v.tensor_scalar(rc, rb, 1.0, None, ALU.add), lnin_ready)
            link(v.scalar_tensor_tensor(ra, rc, -1.0, rb, ALU.add, ALU.subtract))
            link(v.reciprocal(hot(0), rc))
            link(v.scalar_tensor_tensor(ra, ra, -1.0, hot(0), ALU.mult, ALU.mult))
            link(v.scalar_tensor_tensor(ra, logit, 0.0, ra, ALU.max, ALU.add))
            dve.wait_ge(ln_ready, 1)
            v.scalar_tensor_tensor(rb, hot(1), 2e-35, ra, ALU.max, ALU.add).then_inc(sp_ready, 1)
            dve.wait_ge(sqrt_ready, 1)
            link(v.reciprocal(rc, ra))
            link(v.tensor_tensor(rc, rc, rb, ALU.mult))
            link(v.tensor_tensor(ra, ra, rc, ALU.add))
            link(v.tensor_scalar(ra, ra, 0.5, None, ALU.mult))
            score = ra
            link(v.tensor_tensor(rb, score, ebias[:, :].unsqueeze(1).to_broadcast([P, NT, E]), ALU.add))
            for t in range(NT):
                last = v.max(top[:, t, :], rb[:, t, :])
            link(last)
            for t in range(NT):
                last = v.max_index(topi[:, t, :], top[:, t, :], rb[:, t, :])
            link(last)
            link(v.tensor_copy(topf[:, :, :], topi[:, :, :]))
            item = cst[:, C_ITEM:C_ITEM + E].unsqueeze(1).to_broadcast([P, NT, E])
            for k in range(K):
                last = v.tensor_tensor(hot(k), item, topf[:, :, k:k + 1].to_broadcast([P, NT, E]), ALU.is_equal)
            link(last)
            link(v.tensor_tensor(rc, hot(0), hot(1), ALU.add))
            for k in range(2, K - 1):
                link(v.tensor_tensor(rc, rc, hot(k), ALU.add))
            link(v.tensor_tensor(sel_b[:, :, :], rc, hot(K - 1), ALU.add))
            v.memset(before_b[:, 0, :], 0.0)
            link(v.tensor_copy(before_b[:, 1, :], sel_b[:, 0, :]))
            for t in range(2, NT - 1):
                link(v.tensor_tensor(before_b[:, t, :], before_b[:, t - 1, :], sel_b[:, t - 1, :], ALU.add))
            v.tensor_tensor(before_b[:, NT - 1, :], before_b[:, NT - 2, :], sel_b[:, NT - 2, :], ALU.add).then_inc(sel_ready, 1)
            for k in range(K):
                link(v.tensor_tensor(rc, hot(k), score, ALU.mult))
                link(v.tensor_reduce(wk[:, k, :], rc, AX.X, ALU.add))
            dve.wait_ge(pos_ready, 1)
            link(v.tensor_scalar(rb, p_pos, float(CAP), FAR, ALU.is_ge, ALU.mult))
            link(v.tensor_tensor(rb, p_pos, rb, ALU.add))
            link(v.tensor_tensor(rb, rb, cst[:, C_BASE:C_BASE + E].unsqueeze(1).to_broadcast([P, NT, E]), ALU.add))
            for k in range(K):
                link(v.tensor_tensor(rc, hot(k), rb, ALU.mult))
                link(v.tensor_reduce(dk[:, k, :], rc, AX.X, ALU.add))
            v.tensor_copy(scat[:, :, :], dk[:, :, :]).then_inc(route_ready, 1)
            link(v.tensor_tensor(wsum[:, :], wk[:, 0, :], wk[:, 1, :], ALU.add))
            for k in range(2, K):
                link(v.tensor_tensor(wsum[:, :], wsum[:, :], wk[:, k, :], ALU.add))
            link(v.reciprocal(wrec[:, :], wsum[:, :]))
            held = rb.rearrange("p n e -> p (n e)")[:, 0:K * NT].rearrange("p (k n) -> p k n", k=K)
            link(v.tensor_scalar(held, dk[:, :, :], FAR, None, ALU.is_lt))
            link(v.tensor_tensor(wk[:, :, :], wk[:, :, :], held, ALU.mult))
            for k in range(K):
                v.scalar_tensor_tensor(keep["weight"][:, k, :], wk[:, k, :], ROUTE_SCALE, wrec[:, :], ALU.mult, ALU.mult)
            link(v.tensor_tensor(dk[:, :, :], dk[:, :, :], held, ALU.mult))
            link(v.tensor_copy(keep["slot"][:, :, :], dk[:, :, :]))
            def weight_lo(b, count):
                dve.wait_ge(w_hi_ready, count)
                v.tensor_tensor(w_lo[:, b, :], w_raw[:, b, 0:C], w_hi[:, b, :].bitcast(F32), ALU.subtract).then_inc(w_ready, 1)

            def rotate(n, u, scale):
                dve.wait_ge(t2_done, 4 * n + u + 5)
                v.scalar_tensor_tensor(t1[:, u, :], t1[:, u, :], scale, t2[:, u, :],
                                       ALU.mult, ALU.add).then_inc(rot_ready, 1)

            def head(n, b, scale, more):
                for u in range(NG):
                    cols = slice(u * TG, (u + 1) * TG)
                    dve.wait_ge(rot_stored[u], 16 * n + 16)
                    dve.wait_ge(swap_ready, 4 * n + u + 1)
                    v.scalar_tensor_tensor(t1[:, u, :], p_p[:, u, :], w_raw[:, b, C:C + 1], rope[:, 0, cols],
                                           ALU.add, ALU.mult)
                    v.scalar_tensor_tensor(t2[:, u, :], swapped[:, u % 2, :], scale, rope[:, 1, cols],
                                           ALU.mult, ALU.mult).then_inc(t2_done, 1)
                    if u:
                        rotate(n, u - 1, scale)
                    if u == 1 and more:
                        weight_lo(1 - b, n + 2)
                rotate(n, NG - 1, scale)
            dve.wait_ge(rope_loaded, 16)
            dve.sem_inc(t2_done, 4)
            weight_lo(0, 1)
            with dve.Fori(0, HEADS // 2) as i:
                head(2 * i, 0, QSCALE, True)
                head(2 * i + 1, 1, QSCALE, True)
            with dve.Fori(HEADS // 2, PAIRS - 1) as i:
                head(2 * i, 0, 1.0, True)
                head(2 * i + 1, 1, 1.0, True)
            head(ROPED - 2, 0, 1.0, True)
            head(ROPED - 1, 1, 1.0, False)
            dve.wait_ge(shared_hi_ready, 2)
            v.tensor_tensor(sgu_lo[:, :, :], sgu, sgu_hi[:, :, :].bitcast(F32), ALU.subtract)
            v.tensor_tensor(sdn_lo[:, :, :], sdn, sdn_hi[:, :, :].bitcast(F32), ALU.subtract).then_inc(shared_ready, 1)
            for g in range(NG):
                for i in range(NI):
                    dve.wait_ge(silu_ready, NI * g + i + 1)
                    link(v.tensor_tensor(t1[:, i, :], t1[:, i, :], p_p[:, 2 + i, :], ALU.mult))
                    link(v.tensor_scalar(t1[:, i, :], t1[:, i, :], CLIP, -CLIP, ALU.min, ALU.max))
                    if g:
                        dve.wait_ge(down_psum, 4 * g)
                    link(v.tensor_copy(inter_hi[:, i, :], t1[:, i, :]))
                    v.tensor_tensor(inter_lo[:, i, :], t1[:, i, :], inter_hi[:, i, :].bitcast(F32),
                                    ALU.subtract).then_inc(inter_ready, 1)

        @block.tensor
        def _(pe):
            pe.wait_ge(const_loaded, 64)
            for t in range(NT):
                pe.wait_ge(xn_ready, t + 1)
                if t >= 2:
                    pe.wait_ge(xt_ready, t - 1)
                for c in range(NC):
                    last = nc.tensor.transpose(p_t[:, t % 2, c * P:(c + 1) * P], xn[:, t, c * P:(c + 1) * P], ident)
                last.then_inc(xt_psum, 1)
            for t in range(NT):
                pe.wait_ge(xt_ready, t + 1)
                for c in range(NC):
                    a = slice(t * P, (t + 1) * P)
                    last = three_passes(nc, p_logit[:, t, :], xt_hi[:, c, a], xt_lo[:, c, a],
                                        gw_hi[:, c, :], gw_lo[:, c, :], c == 0, c == NC - 1)
            last.then_inc(logits_ready, 1)
            pe.wait_ge(wv_ready, 1)
            for t in range(NT):
                a = slice(t * P, (t + 1) * P)
                if t >= 2:
                    pe.wait_ge(v_evicted, t - 1)
                out = p_v[:, t % 2, :]
                for c in range(NC):
                    three_passes(nc, out, xt_hi[:, c, a], xt_lo[:, c, a], wv_hi[:, c, :], wv_lo[:, c, :], c == 0, False)
                nc.tensor.matmul(out, one_r[:, :], bv_hi[:, :], start=False, stop=False)
                nc.tensor.matmul(out, one_r[:, :], bv_lo[:, :], start=False, stop=True).then_inc(v_psum, 1)
            pe.wait_ge(sel_ready, 1)
            nc.tensor.matmul(p_t[:, 0, :], upper_b[:, :], sel_b[:, :, :], start=True, stop=False)
            nc.tensor.matmul(p_t[:, 0, :], ones_b[:, :], before_b[:, :, :], start=False, stop=True).then_inc(pos_ready, 1)

            def head(n, b):
                pe.wait_ge(w_ready, n + 1)
                for u in range(NG):
                    cols = slice(u * TG, (u + 1) * TG)
                    pe.wait_ge(t2_done, 4 * n + u + 1)
                    for c in range(NC):
                        w = slice(c * HD, (c + 1) * HD)
                        last = three_passes(nc, p_p[:, u, :], w_hi[:, b, w], w_lo[:, b, w],
                                            xt_hi[:, c, cols], xt_lo[:, c, cols], c == 0, c == NC - 1)
                    last.then_inc(qk_psum, 1)
            with pe.Fori(0, PAIRS) as i:
                head(2 * i, 0)
                head(2 * i + 1, 1)
            pe.wait_ge(t2_done, 4 * ROPED + 4)
            pe.wait_ge(shared_ready, 1)

            def gate_up(g):
                cols = slice(g * TG, (g + 1) * TG)
                if g:
                    pe.wait_ge(inter_ready, NI * g)
                for k in range(2 * NI):
                    for c in range(NC):
                        w = slice(k * P, (k + 1) * P)
                        last = three_passes(nc, p_p[:, k, :], sgu_hi[:, c, w], sgu_lo[:, c, w],
                                            xt_hi[:, c, cols], xt_lo[:, c, cols], c == 0, c == NC - 1)
                last.then_inc(gu_psum, 1)
            gate_up(0)
            for g in range(NG):
                pe.wait_ge(inter_ready, NI * (g + 1))
                for r in range(4):
                    t = 4 * g + r
                    if t >= 2:
                        pe.wait_ge(down_evicted, t - 1)
                    for i in range(NI):
                        a = slice(r * P, (r + 1) * P)
                        last = three_passes(nc, p_v[:, t % 2, :], inter_hi[:, i, a], inter_lo[:, i, a],
                                            sdn_hi[:, i, :], sdn_lo[:, i, :], i == 0, i == NI - 1)
                    last.then_inc(down_psum, 1)
                if g + 1 < NG:
                    gate_up(g + 1)


def attend(nc, ins, d, keep):
    UNITS = [4 * (r + 1) for r in range(NG)]
    BEFORE = [sum(UNITS[:r]) for r in range(NG)]
    HU = sum(UNITS)
    JU = G * HU
    JT = JU + G * NG
    SRING, TRING, PRING, NRING = 5, 2, 4, 8
    LAG = 2
    EXP_LAG = 4
    AHEAD = 4 * NG + EXP_LAG + 1
    HOLD = 4
    EXTRA = [4 * a + 3 for a in range(HOLD)]
    with ExitStack() as ctx:
        sb = lambda n, s, dt=F32: ctx.enter_context(nc.sbuf_tensor(n, s, dt))
        ps = lambda n, s: ctx.enter_context(nc.psum_tensor(n, s, F32))
        sem = lambda n: ctx.enter_context(nc.semaphore(n))
        q_raw, k_raw = sb("q_raw", [P, NG, TG]), sb("k_raw", [P, NG, TG])
        v_raw = sb("v_raw", [P, NT, HD])
        q_hi, q_lo = sb("q_hi", [P, T], F32R), sb("q_lo", [P, T], F32R)
        k_hi, k_lo = sb("k_hi", [P, T], F32R), sb("k_lo", [P, T], F32R)
        v_hi, v_lo = sb("v_hi", [P, NT, HD], F32R), sb("v_lo", [P, NT, HD], F32R)
        prob = sb("prob", [P, HU, TG])
        pt_hi, pt_lo = sb("pt_hi", [P, PRING, TG], F32R), sb("pt_lo", [P, PRING, TG], F32R)
        chunk_max, neg_max = sb("chunk_max", [P, NRING, 4]), sb("neg_max", [P, NRING])
        chunk_sum, row_sum = sb("chunk_sum", [P, NG, 4, NG]), sb("row_sum", [P, NG, 4])
        inv_sum = sb("inv_sum", [P, NG, 4])
        inv_cols = sb("inv_cols", [P, 2, TG])
        head_out = sb("head_out", [P, 2, TG])
        ident_b, mask_b = sb("ident_b", [P, P], BF16), sb("mask_b", [P, P], BF16)
        cst = keep["cst"]
        ident, ones = cst[:, C_ID:C_ID + P], cst[:, C_ONES:C_ONES + P]
        p_s, p_t, p_o = ps("p_s", [P, SRING, 512]), ps("p_tr", [P, TRING, 512]), ps("p_o", [P, 512])

        const_ready = sem("const_ready")
        q_loaded = [sem(f"q_loaded{r}") for r in range(NG)]
        k_loaded = [sem(f"k_loaded{r}") for r in range(NG)]
        v_loaded = [sem(f"v_loaded{r}") for r in range(NG)]
        split_hi = sem("split_hi")
        q_split, k_split, v_split = sem("q_split"), sem("k_split"), sem("v_split")
        scores_ready, max_chain, max_ready, exp_done = sem("scores_ready"), sem("max_chain"), sem("max_ready"), sem("exp_done")
        bank_filled, pt_hi_ready, pt_ready = sem("bank_filled"), sem("pt_hi_ready"), sem("pt_ready")
        sum_chain, inv_ready, cols_ready = sem("sum_chain"), sem("inv_ready"), sem("cols_ready")
        pv_done, out_ready = sem("pv_done"), sem("out_ready")
        out_stored = [sem(f"out_stored{b}") for b in range(2)]
        SCORE_CREDIT, PV_CREDIT = HU, 16
        block = ctx.enter_context(nc.Block())
        groups = [(g, r) for g in range(G) for r in range(NG)]

        def rows(g, r):
            return [(i, 16 * g + 4 * r + i, r + 1) for i in range(4)]

        def chunk_index(g, r, i, c):
            return HU * g + BEFORE[r] + i * (r + 1) + c

        def width(r, i, c):
            return TG if c < r else P * (i + 1)

        def unit_index(g, r, k):
            return HU * g + BEFORE[r] + k

        def bank_index(g, r, k):
            order = {UNITS[r]: UNITS[r] - 1, UNITS[r] - 1: UNITS[r]}.get(k, k)
            return HU * g + BEFORE[r] + order + NG * g + r

        def first_row(r, k):
            return max(0, k - 4 * r)

        chunks = [(g, r, i, c) for g in range(G + 1) for r in range(NG) for i in range(4) for c in range(r + 1)]
        opening = [("chunk", *c) for c in chunks[:AHEAD - HOLD]]

        def turns(more):
            made = AHEAD - HOLD
            for u, (g, r, k) in enumerate((g, r, k) for g, r in groups for k in range(UNITS[r])):
                if k == UNITS[r] - 1:
                    yield "sums", g, r, 0
                if k == LAG - 1 and (g, r) != groups[0]:
                    yield "out", *groups[NG * g + r - 1], 0
                yield "unit", g, r, k
                want = u + 1 + AHEAD - HOLD + sum(u >= a for a in EXTRA)
                want = min(want, JU) if u + 1 + AHEAD - HOLD < JU else u + 1 + AHEAD - HOLD
                for c in chunks[made:want] if more or made < JU else []:
                    yield "chunk", *c
                made = max(made, want)
            yield "out", *groups[-1], 0

        def late_chunks():
            return chunks[AHEAD - HOLD - EXP_LAG:AHEAD - HOLD]

        def for_each_head(engine, do):
            with engine.Fori(0, KV - 1) as j:
                do(j, True)
            do(KV - 1, False)

        @block.sync
        def _(sp):
            def load(j, g, r):
                if g == 0:
                    sp.wait_ge(k_split, 4 * j + r + 1)
                    sp.dma_start(k_raw[:, r:r + 1, :], d["qk"][bass.ds(HEADS + j, 1), :, r * TG:(r + 1) * TG]
                                 .rearrange("a p n -> p a n")).then_inc(k_loaded[r], 16)
                sp.wait_ge(q_split, 16 * j + 4 * g + r + 1)
                sp.dma_start(q_raw[:, r:r + 1, :], d["qk"][bass.ds(G * j + g, 1), :, r * TG:(r + 1) * TG]
                             .rearrange("a p n -> p a n")).then_inc(q_loaded[r], 16)
                if g == 0:
                    sp.wait_ge(v_split, 4 * j + r + 1)
                    sp.dma_start(v_raw[:, 4 * r:4 * r + 4, :],
                                 d["v"].rearrange("(n p) c -> p n c", p=P)[:, 4 * r:4 * r + 4, bass.ds(j * HD, HD)])\
                      .then_inc(v_loaded[r], 16)

            with sp.Fori(0, KV) as j:
                for r in range(NG):
                    load(j, 0, r)
                for g, r in groups[NG:]:
                    load(j, g, r)

        @block.gpsimd
        def _(pool):
            def split(hi, lo, raw, done, count):
                blocks = lambda m: m.rearrange("p (a b) -> p a b", b=P) if len(m.shape) == 2 else m
                nc.gpsimd.tensor_tensor(blocks(hi), blocks(raw), ones.unsqueeze(1).to_broadcast([P, TG // P, P]),
                                        ALU.mult).then_inc(split_hi, 1)
                pool.wait_ge(split_hi, count)
                nc.gpsimd.tensor_tensor(lo, raw, hi.bitcast(F32), ALU.subtract).then_inc(done, 1)

            for s in (q_split, k_split, v_split):
                pool.sem_inc(s, 4)
            with pool.Fori(0, KV) as j:
                at = [0]

                def nth():
                    at[0] += 1
                    return 24 * j + at[0]
                for g, r in groups:
                    cols = slice(r * TG, (r + 1) * TG)
                    if g == 0:
                        pool.wait_ge(k_loaded[r], 16 * j + 16)
                        pool.wait_ge(scores_ready, JU * j + SCORE_CREDIT)
                        split(k_hi[:, cols], k_lo[:, cols], k_raw[:, r, :], k_split, nth())
                    pool.wait_ge(q_loaded[r], 64 * j + 16 * g + 16)
                    pool.wait_ge(scores_ready, JU * j + HU * g - HU + BEFORE[r] + UNITS[r] + SCORE_CREDIT)
                    split(q_hi[:, cols], q_lo[:, cols], q_raw[:, r, :], q_split, nth())
                    if g == 1:
                        pool.wait_ge(v_loaded[r], 16 * j + 16)
                        pool.wait_ge(pv_done, JU * j - UNITS[NG - 1] + 4 * r + 4 + PV_CREDIT)
                        split(v_hi[:, 4 * r:4 * r + 4, :], v_lo[:, 4 * r:4 * r + 4, :],
                              v_raw[:, 4 * r:4 * r + 4, :], v_split, nth())

        @block.scalar
        def _(act):
            act.sem_inc(exp_done, SRING)
            for b in range(2):
                act.sem_inc(out_stored[b], 16)

            def head(j, more, begin=False):
                late = [] if begin else late_chunks()

                def exp(g, r, i, c):
                    row, m, w = 16 * g + 4 * r + i, chunk_index(g, r, i, c), width(r, i, c)
                    if c == 0:
                        act.wait_ge(max_ready, 64 * j + row + 1)
                    nc.scalar.activation(prob[:, m % HU, 0:w], p_s[:, m % SRING, 0:w], ACT.Exp,
                                         bias=neg_max[:, row % NRING:row % NRING + 1],
                                         accum_out=chunk_sum[:, r, i, c:c + 1]).then_inc(exp_done, 1)

                def chunk(g, r, i, c):
                    late.append((g, r, i, c))
                    if len(late) > EXP_LAG:
                        exp(*late.pop(0))

                def unit(g, r, k):
                    m, x = unit_index(g, r, k), P * first_row(r, k)
                    act.wait_ge(bank_filled, JT * j + bank_index(g, r, k) + 1)
                    act.wait_ge(pv_done, JU * j + m - PRING + 1 + PV_CREDIT)
                    nc.scalar.activation(pt_hi[:, m % PRING, x:TG], p_t[:, bank_index(g, r, k) % TRING, x:TG], ACT.Copy)\
                      .then_inc(pt_hi_ready, 1)
                    if late and m + AHEAD >= JU and not (more and m + AHEAD - HOLD >= JU):
                        exp(*late.pop(0))
                    if k == LAG + 1 and (g, r) != groups[0]:
                        store(NG * g + r - 1)

                def sums(g, r, _):
                    n = 4 * g + r
                    act.wait_ge(bank_filled, JT * j + bank_index(g, r, UNITS[r]) + 1)
                    act.wait_ge(out_ready, 16 * j + n + 1)
                    nc.scalar.activation(inv_cols[:, n % 2, :], p_t[:, bank_index(g, r, UNITS[r]) % TRING, :], ACT.Copy)\
                      .then_inc(cols_ready, 1)

                def store(n):
                    g, r = groups[n]
                    act.wait_ge(out_ready, 16 * j + n + 1 + 2)
                    nc.scalar.dma_start(d["o"][bass.ds(KV * g + j, 1), :, r * TG:(r + 1) * TG].rearrange("a p n -> p a n"),
                                        head_out[:, n % 2:n % 2 + 1, :]).then_inc(out_stored[n % 2], 16)

                do = {"chunk": chunk, "unit": unit, "sums": sums, "out": lambda *_: None}
                for what, *at in opening if begin else turns(more):
                    do[what](*at)
                if not begin:
                    store(len(groups) - 1)

            head(0, True, begin=True)
            for_each_head(act, head)
            for b in range(2):
                act.wait_ge(out_stored[b], 16 + 16 * KV * len(groups) // 2)

        @block.vector
        def _(dve):
            v = nc.vector
            v.tensor_copy(mask_b[:, :], cst[:, C_MASK:C_MASK + P]).then_inc(const_ready, 1)
            v.tensor_copy(ident_b[:, :], ident).then_inc(const_ready, 1)
            dve.sem_inc(out_ready, 2)

            def head(j, more, begin=False):
                def chunk(g, r, i, c):
                    m, row = chunk_index(g, r, i, c), 16 * g + 4 * r + i
                    dve.wait_ge(scores_ready, JU * j + m + 1 + SCORE_CREDIT)
                    s = p_s[:, m % SRING, 0:width(r, i, c)]
                    nm = neg_max[:, row % NRING:row % NRING + 1]
                    if r == 0:
                        v.tensor_reduce(nm, s, AX.X, ALU.max, negate=True).then_inc(max_ready, 1)
                        return
                    v.tensor_reduce(chunk_max[:, row % NRING, c:c + 1], s, AX.X, ALU.max).then_inc(max_chain, 1)
                    if c == r:
                        made = (HU - UNITS[0]) * (4 * j + g) + BEFORE[r] - UNITS[0] + (i + 1) * (r + 1)
                        dve.wait_ge(max_chain, made)
                        v.tensor_reduce(nm, chunk_max[:, row % NRING, 0:r + 1], AX.X, ALU.max, negate=True).then_inc(max_ready, 1)

                def unit(g, r, k):
                    m, x = unit_index(g, r, k), P * first_row(r, k)
                    if k == 2:
                        inverse(g, r)
                    dve.wait_ge(pt_hi_ready, JU * j + m + 1)
                    v.tensor_tensor(pt_lo[:, m % PRING, x:TG], p_t[:, bank_index(g, r, k) % TRING, x:TG],
                                    pt_hi[:, m % PRING, x:TG].bitcast(F32), ALU.subtract).then_inc(pt_ready, 1)

                def inverse(g, r):
                    n = 4 * g + r
                    dve.wait_ge(exp_done, JU * j + BEFORE[r] + HU * g + UNITS[r] + SRING)
                    v.tensor_reduce(row_sum[:, r, :], chunk_sum[:, r, :, 0:r + 1], AX.X, ALU.add).then_inc(sum_chain, 1)
                    dve.wait_ge(sum_chain, 16 * j + n + 1)
                    v.reciprocal(inv_sum[:, r, :], row_sum[:, r, :]).then_inc(inv_ready, 1)

                def out(g, r, _):
                    n = 4 * g + r
                    dve.wait_ge(cols_ready, 16 * j + n + 1)
                    dve.wait_ge(pv_done, JU * j + unit_index(g, r, UNITS[r] - 1) + 1 + PV_CREDIT)
                    dve.wait_ge(out_stored[n % 2], 16 * (8 * j + n // 2) + 16)
                    v.tensor_tensor(head_out[:, n % 2, :], p_o[:, :], inv_cols[:, n % 2, :], ALU.mult).then_inc(out_ready, 1)

                do = {"chunk": chunk, "unit": unit, "sums": lambda *_: None, "out": out}
                for what, *at in opening if begin else turns(more):
                    do[what](*at)

            head(0, True, begin=True)
            for_each_head(dve, head)

        @block.tensor
        def _(pe):
            pe.wait_ge(const_ready, 2)
            pe.sem_inc(scores_ready, SCORE_CREDIT)
            pe.sem_inc(pv_done, PV_CREDIT)

            def head(j, more, begin=False):
                waiting = []

                def chunk(g, r, i, c):
                    m, w = chunk_index(g, r, i, c), width(r, i, c)
                    if i == 0 and c == 0:
                        pe.wait_ge(q_split, 16 * j + 4 * g + r + 1 + 4)
                        if g % G == 0:
                            pe.wait_ge(k_split, 4 * j + g + r + 1 + 4)
                    pe.wait_ge(exp_done, JU * j + m + 1)
                    a, keys = slice((4 * r + i) * P, (4 * r + i + 1) * P), slice(c * TG, c * TG + w)
                    out = p_s[:, m % SRING, 0:w]
                    nc.tensor.matmul(out, q_hi[:, a], k_hi[:, keys], start=True, stop=False)
                    if c == r:
                        nc.tensor.matmul(p_s[:, m % SRING, w - P:w], ident_b[:, :], mask_b[:, :], start=False, stop=False)
                    nc.tensor.matmul(out, q_hi[:, a], k_lo[:, keys], start=False, stop=False)
                    nc.tensor.matmul(out, q_lo[:, a], k_hi[:, keys], start=False, stop=True).then_inc(scores_ready, 1)

                def multiply(g, r, k):
                    m, x = unit_index(g, r, k), P * first_row(r, k)
                    if g == 0 and k % 4 == 0 and k // 4 == r:
                        pe.wait_ge(v_split, 4 * j + r + 1 + 4)
                    if k == 0:
                        pe.wait_ge(out_ready, 16 * j + 4 * g + r + 2)
                    pe.wait_ge(pt_ready, JU * j + m + 1)
                    last = three_passes(nc, p_o[:, x:TG], v_hi[:, k, :], v_lo[:, k, :],
                                        pt_hi[:, m % PRING, x:TG], pt_lo[:, m % PRING, x:TG], k == 0, k == UNITS[r] - 1)
                    last.then_inc(pv_done, 1)

                def bank_free(b):
                    g, r, k = next((g, r, k) for g, r in groups for k in range(UNITS[r] + 1)
                                   if bank_index(g, r, k) == b - TRING)
                    if k < UNITS[r]:
                        return pt_ready, JU * j + unit_index(g, r, k) + 1
                    return cols_ready, 16 * j + 4 * g + r + 1

                def unit(g, r, k):
                    b = bank_index(g, r, k)
                    if b >= TRING:
                        pe.wait_ge(*bank_free(b))
                    for i in range(first_row(r, k), 4):
                        if k == 0:
                            pe.wait_ge(exp_done, JU * j + chunk_index(g, r, i, r) + 1 + SRING)
                        last = nc.tensor.transpose(p_t[:, b % TRING, i * P:(i + 1) * P], 
                                                   prob[:, chunk_index(0, r, i, k // 4), k % 4 * P:(k % 4 + 1) * P], ident)
                    last.then_inc(bank_filled, 1)
                    waiting.append((g, r, k))
                    if len(waiting) > LAG:
                        multiply(*waiting.pop(0))

                def sums(g, r, _):
                    b = bank_index(g, r, UNITS[r])
                    pe.wait_ge(inv_ready, 16 * j + 4 * g + r + 1)
                    pe.wait_ge(*bank_free(b))
                    for i in range(4):
                        last = nc.tensor.transpose(p_t[:, b % TRING, i * P:(i + 1) * P],
                                                   inv_sum[:, r, i:i + 1].to_broadcast([P, P]), ident)
                    last.then_inc(bank_filled, 1)

                do = {"chunk": chunk, "unit": unit, "sums": sums, "out": lambda *_: None}
                for what, *at in opening if begin else turns(more):
                    do[what](*at)
                while waiting:
                    multiply(*waiting.pop(0))

            head(0, True, begin=True)
            for_each_head(pe, head)


def turn(nc, tick, source, turned, n):
    nc.gpsimd.wait_ge(turned, n + 1)
    nc.gpsimd.tensor_tensor(tick[:, :], source[0:1, 0:1], source[0:1, 0:1], ALU.mult).then_inc(turned, 1)


def experts(nc, ins, d, keep):
    with ExitStack() as ctx:
        sb = lambda n, s, dt=F32: ctx.enter_context(nc.sbuf_tensor(n, s, dt))
        ps = lambda n, s: ctx.enter_context(nc.psum_tensor(n, s, F32))
        sem = lambda n: ctx.enter_context(nc.semaphore(n))
        both = lambda n: [sem(f"{n}{b}") for b in range(2)]
        index = sb("index", [HALF, 2, 2], U32)
        rows, tick = sb("rows", [HALF, 2, 2, C]), sb("tick", [1, 1])
        gu_raw, dn_raw = sb("gu_raw", [P, 2, NC, 2 * I]), sb("dn_raw", [P, 2, NI, C])
        gu_hi, gu_lo = sb("gu_hi", [P, 2, NC, 2 * I], F32R), sb("gu_lo", [P, 2, NC, 2 * I], F32R)
        dn_hi, dn_lo = sb("dn_hi", [P, 2, NI, C], F32R), sb("dn_lo", [P, 2, NI, C], F32R)
        et_hi, et_lo = sb("et_hi", [P, 2, 2, 2 * CAP], F32R), sb("et_lo", [P, 2, 2, 2 * CAP], F32R)
        silu, inner = sb("silu", [P, 2, NI * CAP]), sb("inner", [P, 2, NI * CAP])
        in_hi, in_lo = sb("in_hi", [P, 2, NI, CAP], F32R), sb("in_lo", [P, 2, NI, CAP], F32R)
        rows_out = sb("rows_out", [HALF, 2, 2, C])
        wo_raw = sb("wo_raw", [P, 1, C])
        wo_hi, wo_lo = keep["wo_hi"], keep["wo_lo"]
        ident = keep["cst"][0:HALF, C_ID:C_ID + HALF]
        ones = keep["cst"][:, C_ONES:C_ONES + P]
        p_x, p_gu, p_y = ps("p_x", [P, 2, 512]), ps("p_gu", [P, 2, 2, 512]), ps("p_y", [P, 2, 512])

        index_loaded, gathered, w_loaded, stored = (both(n) for n in ("index_loaded", "gathered", "ew_loaded", "stored"))
        wo_loaded, wo_hi_ready, wo_ready = sem("wo_loaded"), sem("wo_hi_ready"), sem("wo_ready")
        gu_hi_ready, gu_ready = sem("gu_hi_ready"), sem("gu_ready")
        dn_hi_ready, dn_ready = sem("dn_hi_ready"), sem("dn_ready")
        x_psum, et_hi_ready, et_ready = sem("x_psum"), sem("et_hi_ready"), sem("et_ready")
        gu_done, silu_ready, inner_ready, in_hi_ready, in_ready = (
            sem(n) for n in ("gu_done", "esilu_ready", "inner_ready", "in_hi_ready", "in_ready"))
        y_done, y_evicted, turned = sem("y_done"), sem("y_evicted"), sem("turned")
        block = ctx.enter_context(nc.Block())
        PAIRS = E // 2 - 2
        CR = 2

        @block.sync
        def _(sp):
            def load(e, b):
                if not isinstance(e, int):
                    sp.wait_ge(gathered[b], 16 * (e - b))
                for h in range(2):
                    sp.dma_start(index[:, b, h:h + 1], d["slot_token"][bass.ds(e * CAP + h * HALF, HALF), :])\
                      .then_inc(index_loaded[b], 16)
                sp.wait_ge(gu_ready, e + 1)
                sp.dma_start(gu_raw[:, b, :, :], ins["wgu"][bass.ds(e, 1)].rearrange("e p c n -> p (e c) n")).then_inc(w_loaded[b], 16)
                sp.wait_ge(dn_ready, e + 1)
                sp.dma_start(dn_raw[:, b, :, :], ins["wdn"][bass.ds(e, 1)].rearrange("e p c n -> p (e c) n")).then_inc(w_loaded[b], 16)
            load(0, 0)
            load(1, 1)
            sp.dma_start(wo_raw[:, :, :], ins["wo"][:, HEADS - 1:HEADS, :]).then_inc(wo_loaded, 16)
            with sp.Fori(0, E // 2 - 1) as i:
                for b in range(2):
                    load(2 * i + b + 2, b)
                sp.wait_ge(wo_ready, i + 1)
                sp.dma_start(wo_raw[:, :, :], ins["wo"][:, bass.ds(i, 1), :]).then_inc(wo_loaded, 16)
            for b in range(2):
                sp.wait_ge(stored[b], 16 * (E // 2) + 16)

        @block.gpsimd
        def _(pool):
            def gather(e, b):
                pool.wait_ge(x_psum, e + 1)
                pool.wait_ge(index_loaded[b], 16 * (e - b) + 32)
                turn(nc, tick, ones, turned, e)
                for h in range(2):
                    pool.indirect_dma_start(rows[:, b, h, :], None, d["xn"],
                                            bass.IndirectOffsetOnAxis(ap=index[:, b, h:h + 1], axis=0),
                                            bounds_check=T - 1, oob_is_err=False).then_inc(gathered[b], 16)

            def split_down(e, b):
                pool.wait_ge(w_loaded[b], 16 * (e - b) + 32)
                pool.wait_ge(y_done, e + 1)
                blocks = lambda m: m.rearrange("p a (u v) -> p (a u) v", v=P)
                nc.gpsimd.tensor_tensor(blocks(dn_hi[:, b, :, :]), blocks(dn_raw[:, b, :, :]),
                                        ones.unsqueeze(1).to_broadcast([P, NI * C // P, P]), ALU.mult).then_inc(dn_hi_ready, 1)
                pool.wait_ge(dn_hi_ready, e + 1)
                nc.gpsimd.tensor_tensor(dn_lo[:, b, :, :], dn_raw[:, b, :, :], dn_hi[:, b, :, :].bitcast(F32),
                                        ALU.subtract).then_inc(dn_ready, 1)
            pool.sem_inc(dn_ready, CR)
            pool.sem_inc(turned, 1)
            gather(0, 0)
            gather(1, 1)
            with pool.Fori(0, E // 2 - 1) as i:
                for b in range(2):
                    split_down(2 * i + b, b)
                    gather(2 * i + b + 2, b)
            split_down(E - 2, 0)
            split_down(E - 1, 1)



        @block.scalar
        def _(act):
            def weights(e, b):
                act.wait_ge(w_loaded[b], 16 * (e - b) + 32)
                act.wait_ge(gu_done, e + 1)
                nc.scalar.activation(gu_hi[:, b, :, :], gu_raw[:, b, :, :], ACT.Copy).then_inc(gu_hi_ready, 1)

            def tokens(e, b):
                act.wait_ge(x_psum, e + 1 + CR)
                nc.scalar.activation(et_hi[:, b, :, :], p_x[:, :, 0:2 * CAP], ACT.Copy).then_inc(et_hi_ready, 1)

            def gate(e, b):
                act.wait_ge(gu_done, e + 1 + CR)
                nc.scalar.activation(silu[:, b, :], p_gu[:, b, 0, 0:NI * CAP], ACT.Silu).then_inc(silu_ready, 1)

            def evict(e, b):
                act.wait_ge(y_done, e + 1 + CR)
                act.wait_ge(stored[b], 8 * (e - b) + 16)
                nc.scalar.activation(rows_out[:, b, :, :], p_y[0:HALF, :, :], ACT.Copy).then_inc(y_evicted, 1)

            def store(e, b):
                act.wait_ge(y_evicted, e + 1 + 1)
                act.dma_start(d["expert"].rearrange("(e h p) c -> e p h c", h=2, p=HALF)[bass.ds(e, 1)]
                              .rearrange("e p h c -> p (e h) c"), rows_out[:, b, :, :]).then_inc(stored[b], 16)

            def project_weights(h, count):
                act.wait_ge(wo_loaded, 16 * count)
                nc.scalar.activation(wo_hi[:, bass.ds(h, 1), :], wo_raw[:, :, :], ACT.Copy).then_inc(wo_hi_ready, 1)
            for b in range(2):
                act.sem_inc(stored[b], 16)
            act.sem_inc(y_evicted, 1)
            def step(e, b, weights_ahead, tokens_ahead):
                gate(e, b)
                if tokens_ahead:
                    tokens(e + 1, 1 - b)
                if weights_ahead:
                    weights(e + 2, b)
                evict(e - 1, 1 - b)
                store(e - 1, 1 - b)
            weights(0, 0)
            tokens(0, 0)
            weights(1, 1)
            gate(0, 0)
            tokens(1, 1)
            weights(2, 0)
            project_weights(HEADS - 1, 1)
            with act.Fori(0, PAIRS) as i:
                step(2 * i + 1, 1, True, True)
                project_weights(i, i + 2)
                step(2 * i + 2, 0, True, True)
            step(E - 3, 1, True, True)
            project_weights(HEADS - 2, HEADS)
            step(E - 2, 0, False, True)
            step(E - 1, 1, False, False)
            evict(E - 1, 1)
            store(E - 1, 1)

        @block.vector
        def _(dve):
            v = nc.vector

            def weights(e, b):
                dve.wait_ge(gu_hi_ready, e + 1)
                v.tensor_tensor(gu_lo[:, b, :, :], gu_raw[:, b, :, :], gu_hi[:, b, :, :].bitcast(F32), ALU.subtract)\
                 .then_inc(gu_ready, 1)

            def tokens(e, b):
                dve.wait_ge(et_hi_ready, e + 1)
                v.tensor_tensor(et_lo[:, b, :, :], p_x[:, :, 0:2 * CAP], et_hi[:, b, :, :].bitcast(F32), ALU.subtract)\
                 .then_inc(et_ready, 1)

            def gate(e, b):
                dve.wait_ge(silu_ready, e + 1)
                v.tensor_tensor(inner[:, b, :], silu[:, b, :], p_gu[:, b, 1, 0:NI * CAP], ALU.mult).then_inc(inner_ready, 1)
                dve.wait_ge(inner_ready, e + 1)
                dve.wait_ge(y_done, e + 1)
                flat = lambda m: m[:, b, :, :].rearrange("p i n -> p (i n)")
                v.tensor_copy(flat(in_hi), inner[:, b, :]).then_inc(in_hi_ready, 1)
                dve.wait_ge(in_hi_ready, e + 1)
                v.tensor_tensor(flat(in_lo), inner[:, b, :], flat(in_hi).bitcast(F32), ALU.subtract).then_inc(in_ready, 1)

            def project_weights(h, count):
                dve.wait_ge(wo_hi_ready, count)
                v.tensor_tensor(wo_lo[:, bass.ds(h, 1), :], wo_raw[:, :, :],
                                wo_hi[:, bass.ds(h, 1), :].bitcast(F32), ALU.subtract).then_inc(wo_ready, 1)
            dve.sem_inc(gu_ready, CR)
            def step(e, b, weights_ahead, tokens_ahead):
                if tokens_ahead:
                    tokens(e + 1, 1 - b)
                gate(e, b)
                if weights_ahead:
                    weights(e + 2, b)
            weights(0, 0)
            tokens(0, 0)
            weights(1, 1)
            step(0, 0, True, True)
            project_weights(HEADS - 1, 1)
            with dve.Fori(0, PAIRS) as i:
                step(2 * i + 1, 1, True, True)
                project_weights(i, i + 2)
                step(2 * i + 2, 0, True, True)
            step(E - 3, 1, True, True)
            project_weights(HEADS - 2, HEADS)
            step(E - 2, 0, False, True)
            step(E - 1, 1, False, False)
            dve.wait_ge(wo_ready, HEADS)

        @block.tensor
        def _(pe):
            def tokens(e, b):
                pe.wait_ge(gathered[b], 16 * (e - b) + 32)
                if isinstance(e, int) and e == 0:
                    pass
                else:
                    pe.wait_ge(et_ready, e)
                for c in range(NC):
                    for h in range(2):
                        x = (c % 2) * CAP + h * HALF
                        last = nc.tensor.transpose(p_x[:, c // 2, x:x + HALF], rows[:, b, h, c * P:(c + 1) * P], ident)
                last.then_inc(x_psum, 1)

            def gate_up(e, b):
                pe.wait_ge(gu_ready, e + 1 + CR)
                pe.wait_ge(et_ready, e + 1)
                pe.wait_ge(in_ready, e + 1)
                for k in range(2 * NI):
                    x = (k % NI) * CAP
                    for c in range(NC):
                        w, t = slice(k * P, (k + 1) * P), slice((c % 2) * CAP, (c % 2 + 1) * CAP)
                        last = three_passes(nc, p_gu[:, b, k // NI, x:x + CAP], gu_hi[:, b, c, w], gu_lo[:, b, c, w],
                                            et_hi[:, b, c // 2, t], et_lo[:, b, c // 2, t], c == 0, c == NC - 1)
                last.then_inc(gu_done, 1)

            def down(e, b):
                pe.wait_ge(dn_ready, e + 1 + CR)
                pe.wait_ge(in_ready, e + 1 + CR)
                pe.wait_ge(y_evicted, e + 1)
                for h in range(2):
                    for i in range(NI):
                        a = slice(h * HALF, (h + 1) * HALF)
                        last = three_passes(nc, p_y[0:HALF, h, :], in_hi[:, b, i, a], in_lo[:, b, i, a],
                                            dn_hi[:, b, i, :], dn_lo[:, b, i, :], i == 0, i == NI - 1)
                last.then_inc(y_done, 1)
            pe.sem_inc(x_psum, CR)
            pe.sem_inc(gu_done, CR)
            pe.sem_inc(y_done, CR)
            pe.sem_inc(in_ready, CR)
            def step(e, b, tokens_ahead):
                gate_up(e, b)
                if tokens_ahead:
                    tokens(e + 1, 1 - b)
                down(e - 1, 1 - b)
            tokens(0, 0)
            gate_up(0, 0)
            tokens(1, 1)
            with pe.Fori(0, PAIRS) as i:
                step(2 * i + 1, 1, True)
                step(2 * i + 2, 0, True)
            step(E - 3, 1, True)
            step(E - 2, 0, True)
            step(E - 1, 1, False)
            down(E - 1, 1)


def combine(nc, ins, d, keep, out):
    with ExitStack() as ctx:
        sb = lambda n, s, dt=F32: ctx.enter_context(nc.sbuf_tensor(n, s, dt))
        sem = lambda n: ctx.enter_context(nc.semaphore(n))
        both = lambda n: [sem(f"{n}{b}") for b in range(2)]
        o_raw = sb("o_raw", [P, 2, HEADS, P])
        o_hi, o_lo = sb("o_hi", [P, 2, HEADS, P], F32R), sb("o_lo", [P, 2, HEADS, P], F32R)
        chosen = sb("chosen", [P, 2, K, C])
        shared, x = sb("shared", [P, 2, C]), sb("x_in", [P, 2, C])
        mixed, gate, result = sb("mixed", [P, 2, C]), sb("gate", [P, 2, C]), sb("result", [P, 2, C])
        bias, tick = sb("bias", [P, C]), sb("tick_c", [1, 1])
        slot = sb("slot_now", [P, 2, K], U32)
        wo_hi, wo_lo = keep["wo_hi"], keep["wo_lo"]
        p_s = ctx.enter_context(nc.psum_tensor("p_proj", [P, 2, 512], F32))
        o_loaded, row_loaded, chosen_loaded, written = (both(n) for n in ("o_loaded", "row_loaded", "chosen_loaded", "written"))
        bias_loaded, slot_ready, turned = sem("bias_loaded"), sem("slot_ready"), sem("turned_c")
        o_hi_ready, o_ready, s_done = sem("o_hi_ready"), sem("o_ready"), sem("s_done")
        mix_chain, gate_ready, end_chain, result_ready = sem("mix_chain"), sem("gate_ready"), sem("end_chain"), sem("result_ready")
        block = ctx.enter_context(nc.Block())
        CR = 2

        @block.sync
        def _(sp):
            def load_heads(t, b):
                sp.wait_ge(o_ready, t + 1)
                sp.dma_start(o_raw[:, b, :, :], d["o"].rearrange("h p n -> p h n")[:, :, bass.ds(t * P, P)]).then_inc(o_loaded[b], 16)

            def load_rows(t, b):
                sp.wait_ge(result_ready, t + 1)
                sp.dma_start(shared[:, b, :], d["shared"][bass.ds(t * P, P), :]).then_inc(row_loaded[b], 16)
                sp.dma_start(x[:, b, :], ins["x"][bass.ds(t * P, P), :]).then_inc(row_loaded[b], 16)

            def store(t, b):
                sp.wait_ge(result_ready, t + 1 + CR)
                sp.dma_start(out[bass.ds(t * P, P), :], result[:, b, :]).then_inc(written[b], 16)
            for b in range(2):
                load_heads(b, b)
                load_rows(b, b)
            sp.dma_start(bias[:, :], ins["bo"][0].partition_broadcast(P)).then_inc(bias_loaded, 16)
            with sp.Fori(0, NT // 2 - 1) as i:
                for b in range(2):
                    load_heads(2 * i + b + 2, b)
                    store(2 * i + b, b)
                    load_rows(2 * i + b + 2, b)
            for b in range(2):
                store(NT - 2 + b, b)
            for b in range(2):
                sp.wait_ge(written[b], 8 * NT + 16)

        @block.gpsimd
        def _(pool):
            pool.sem_inc(turned, 1)
            with pool.Fori(0, NT // 2) as i:
                for b in range(2):
                    pool.wait_ge(slot_ready, 2 * i + b + 1)
                    turn(nc, tick, keep["cst"], turned, 2 * i + b)
                    for k in range(K):
                        pool.indirect_dma_start(chosen[:, b, k, :], None, d["expert"],
                                                bass.IndirectOffsetOnAxis(ap=slot[:, b, k:k + 1], axis=0),
                                                bounds_check=E * CAP - 1, oob_is_err=False).then_inc(chosen_loaded[b], 16)

        @block.scalar
        def _(act):
            def tile(t, b):
                act.wait_ge(o_loaded[b], 8 * (t - b) + 16)
                act.wait_ge(s_done, t + 1)
                nc.scalar.activation(o_hi[:, b, :, :], o_raw[:, b, :, :], ACT.Copy).then_inc(o_hi_ready, 1)

            def gates(t, b):
                act.wait_ge(mix_chain, K * t + K)
                nc.scalar.activation(gate[:, b, :], mixed[:, b, :], ACT.Silu).then_inc(gate_ready, 1)
            for b in range(2):
                act.sem_inc(written[b], 16)
            with act.Fori(0, NT // 2) as i:
                for b in range(2):
                    tile(2 * i + b, b)
                    gates(2 * i + b, b)

        @block.vector
        def _(dve):
            v = nc.vector

            def tile(t, b, ahead):
                dve.wait_ge(o_hi_ready, t + 1)
                v.tensor_tensor(o_lo[:, b, :, :], o_raw[:, b, :, :], o_hi[:, b, :, :].bitcast(F32), ALU.subtract).then_inc(o_ready, 1)
                dve.wait_ge(row_loaded[b], 16 * (t - b) + 32)
                dve.wait_ge(chosen_loaded[b], 8 * K * (t - b) + 16 * K)
                for k in range(K):
                    if k:
                        dve.wait_ge(mix_chain, K * t + k)
                    v.scalar_tensor_tensor(mixed[:, b, :], chosen[:, b, k, :], keep["weight"][:, k, bass.ds(t, 1)],
                                           mixed[:, b, :] if k else shared[:, b, :], ALU.mult, ALU.add).then_inc(mix_chain, 1)
                if ahead:
                    next_slots(t + 2, b)

            def next_slots(t, b):
                if not (isinstance(t, int) and t < 2):
                    dve.wait_ge(mix_chain, K * (t - 1))
                v.tensor_copy(slot[:, b, :], keep["slot"][:, :, bass.ds(t, 1)].rearrange("p k t -> p (k t)")).then_inc(slot_ready, 1)

            def finish(t, b):
                dve.wait_ge(s_done, t + 1 + CR)
                dve.wait_ge(written[b], 8 * (t - b) + 16)
                v.tensor_tensor(result[:, b, :], p_s[:, b, :], bias[:, :], ALU.add).then_inc(end_chain, 1)
                dve.wait_ge(end_chain, 2 * t + 1)
                dve.wait_ge(gate_ready, t + 1)
                v.tensor_tensor(result[:, b, :], result[:, b, :], gate[:, b, :], ALU.mult).then_inc(end_chain, 1)
                dve.wait_ge(end_chain, 2 * t + 2)
                v.tensor_tensor(result[:, b, :], result[:, b, :], x[:, b, :], ALU.add).then_inc(result_ready, 1)
            dve.sem_inc(o_ready, CR)
            dve.sem_inc(result_ready, CR)
            dve.wait_ge(bias_loaded, 16)
            next_slots(0, 0)
            next_slots(1, 1)
            tile(0, 0, True)
            with dve.Fori(0, NT // 2 - 2) as i:
                tile(2 * i + 1, 1, True)
                finish(2 * i, 0)
                tile(2 * i + 2, 0, True)
                finish(2 * i + 1, 1)
            tile(NT - 3, 1, True)
            finish(NT - 4, 0)
            tile(NT - 2, 0, False)
            finish(NT - 3, 1)
            tile(NT - 1, 1, False)
            finish(NT - 2, 0)
            finish(NT - 1, 1)

        @block.tensor
        def _(pe):
            pe.sem_inc(s_done, CR)
            with pe.Fori(0, NT // 2) as i:
                for b in range(2):
                    t = 2 * i + b
                    pe.wait_ge(o_ready, t + 1 + CR)
                    pe.wait_ge(result_ready, t + 1)
                    for h in range(HEADS):
                        last = three_passes(nc, p_s[:, b, :], o_hi[:, b, h, :], o_lo[:, b, h, :],
                                            wo_hi[:, h, :], wo_lo[:, h, :], h == 0, h == HEADS - 1)
                    last.then_inc(s_done, 1)


def build(nc, ins, out):
    d = {
        "xn": nc.dram_tensor("xn_rows", (T, C), F32).ap(),
        "qk": nc.dram_tensor("qk_heads", (ROPED, P, T), F32).ap(),
        "v": nc.dram_tensor("v_rows", (T, KV * HD), F32).ap(),
        "o": nc.dram_tensor("o_heads", (HEADS, P, T), F32).ap(),
        "slot_token": nc.dram_tensor("slot_token", (E * CAP, 1), U32).ap(),
        "expert": nc.dram_tensor("expert_rows", (E * CAP, C), F32).ap(),
        "shared": nc.dram_tensor("shared_rows", (T, C), F32).ap(),
    }
    with ExitStack() as ctx:
        sb = lambda n, s, dt=F32: ctx.enter_context(nc.sbuf_tensor(n, s, dt))
        keep = {"cst": sb("cst", [P, C_END]), "slot": sb("slot", [P, K, NT], U32), "weight": sb("weight", [P, K, NT])}
        project(nc, ins, d, keep)
        nc.disable_value_cache = True
        attend(nc, ins, d, keep)
        keep["wo_hi"], keep["wo_lo"] = sb("wo_hi", [P, HEADS, C], F32R), sb("wo_lo", [P, HEADS, C], F32R)
        experts(nc, ins, d, keep)
        combine(nc, ins, d, keep, out)


def lay_out(L0_attn_x, L0_attn_Wq, L0_attn_bq, L0_attn_Wk, L0_attn_bk, L0_attn_Wv, L0_attn_bv, L0_attn_Wo,
            L0_attn_bo, L0_ffn_gate_w, L0_ffn_bias, L0_ffn_w_gate, L0_ffn_w_up, L0_ffn_w_down, L0_ffn_sg,
            L0_ffn_su, L0_ffn_sd):
    a = np.ascontiguousarray
    split = np.concatenate([np.arange(0, HD, 2), np.arange(1, HD, 2)])
    wq = np.asarray(L0_attn_Wq).reshape(C, G, KV, HD).transpose(2, 1, 0, 3).reshape(HEADS, C, HD)
    wk = np.asarray(L0_attn_Wk).reshape(C, KV, HD).transpose(1, 0, 2)
    w = np.concatenate([wq, wk])[:, :, split]
    bq = np.asarray(L0_attn_bq).reshape(G, KV, HD).transpose(1, 0, 2).reshape(HEADS, HD)
    b = np.concatenate([bq, np.asarray(L0_attn_bk).reshape(KV, HD)])[:, split]
    wqk = np.concatenate([w.reshape(ROPED, NC, P, HD).transpose(0, 2, 1, 3).reshape(ROPED, P, NC * HD),
                          b[:, :, None]], axis=2)

    def rows(m):
        m = np.swapaxes(np.asarray(m), -1, -2)
        m = m.reshape(*m.shape[:-2], m.shape[-2] // P, P, m.shape[-1])
        return np.swapaxes(m, -3, -2)
    return {
        "x": a(np.asarray(L0_attn_x).reshape(T, C)),
        "wqk": a(wqk),
        "wv": a(rows(np.asarray(L0_attn_Wv).T)),
        "bv": a(np.asarray(L0_attn_bv).reshape(1, -1)),
        "wo": a(rows(np.asarray(L0_attn_Wo).T)),
        "bo": a(np.asarray(L0_attn_bo).reshape(1, -1)),
        "gate_w": a(rows(L0_ffn_gate_w)),
        "ebias": a(np.asarray(L0_ffn_bias)),
        "wgu": a(np.concatenate([rows(L0_ffn_w_gate), rows(L0_ffn_w_up)], axis=3)),
        "wdn": a(rows(L0_ffn_w_down)),
        "sgu": a(np.concatenate([rows(L0_ffn_sg), rows(L0_ffn_su)], axis=2)),
        "sdn": a(rows(L0_ffn_sd)),
        "cst": constant_table(),
        "rope": rope_table(),
        "tok": (np.arange(NT, dtype=np.uint32)[None, :] * P + np.arange(P, dtype=np.uint32)[:, None]).astype(np.uint32),
    }


def kernel(**inputs):
    import concourse.bacc as bacc
    from concourse.bass_utils import run_bass_kernel_spmd

    nc = bacc.Bacc("TRN2", target_bir_lowering=False, num_devices=1)
    arrays = lay_out(**inputs)
    ins = {n: nc.dram_tensor(f"in_{n}", v.shape, mybir.dt.from_np(v.dtype), kind="ExternalInput").ap()
           for n, v in arrays.items()}
    out = nc.dram_tensor("out", (T, C), F32, kind="ExternalOutput").ap()
    build(nc, ins, out)
    r = run_bass_kernel_spmd(nc, [{f"in_{n}": v for n, v in arrays.items()}], core_ids=[0])
    return r.results[0]["out"].reshape(1, T, C)
```

```python
from contextlib import ExitStack

import numpy as np

import concourse.bass as bass
from concourse import mybir

F32 = mybir.dt.float32
F32R = mybir.dt.float32r
BF16 = mybir.dt.bfloat16
U32 = mybir.dt.uint32
ACT = mybir.ActivationFunctionType
ALU = mybir.AluOpType
AX = mybir.AxisListType

P = 128
T, C = 2048, 512
HEADS, KV, HD = 16, 4, 128
G = HEADS // KV
E, K, CAP = 32, 6, 192
I = 256
NT, NC = T // P, C // P
TG, NG = 512, T // 512
NI = I // P
HALF = CAP // 2
ROUTE_SCALE = 1.5
CLIP = 10.0
EPS = 1e-5
FAR = float(1 << 20)
QSCALE = HEADS ** -0.5
ROPED = HEADS + KV

C_ID, C_MASK, C_UPPER, C_ONES, C_ITEM, C_BASE = 0, 128, 256, 384, 512, 544
C_END = 576


def constant_table():
    t = np.zeros((P, C_END), np.float32)
    t[:, C_ID:C_ID + P] = np.eye(P)
    t[:, C_MASK:C_MASK + P] = np.triu(np.full((P, P), -1e30), 1)
    t[:, C_UPPER:C_UPPER + P] = np.triu(np.ones((P, P)), 1)
    t[:, C_ONES:C_ONES + P] = 1.0
    t[:, C_ITEM:C_ITEM + E] = np.arange(E)
    t[:, C_BASE:C_BASE + E] = np.arange(E) * CAP
    return t


def rope_table():
    half = np.arange(0, HD, 2, dtype=np.float32) / np.float32(HD)
    theta = np.float32(1.0) / (np.float64(10000.0) ** half).astype(np.float32)
    freq = (theta[:, None] * np.arange(T, dtype=np.float32)[None, :]).astype(np.float64)
    cos, sin = np.cos(freq).astype(np.float32), np.sin(freq).astype(np.float32)
    return np.stack([np.concatenate([cos, cos]), np.concatenate([-sin, sin])], axis=1).copy()


def three_passes(nc, out, a_hi, a_lo, b_hi, b_lo, first, last):
    nc.tensor.matmul(out, a_hi, b_hi, start=first, stop=False)
    nc.tensor.matmul(out, a_hi, b_lo, start=False, stop=False)
    return nc.tensor.matmul(out, a_lo, b_hi, start=False, stop=last)


def project(nc, ins, d, keep):
    with ExitStack() as ctx:
        sb = lambda n, s, dt=F32: ctx.enter_context(nc.sbuf_tensor(n, s, dt))
        sem = lambda n: ctx.enter_context(nc.semaphore(n))
        xn = sb("xn", [P, NT, C])
        xt_hi, xt_lo = sb("xt_hi", [P, NC, T], F32R), sb("xt_lo", [P, NC, T], F32R)
        wv = sb("wv", [P, NC, C])
        wv_hi, wv_lo = sb("wv_hi", [P, NC, C], F32R), sb("wv_lo", [P, NC, C], F32R)
        bv = sb("bv_row", [1, C])
        bv_hi, bv_lo = sb("bv_hi", [1, C], F32R), sb("bv_lo", [1, C], F32R)
        one_r = keep["one_r"]
        bo = sb("bo_row", [1, C])
        gw = sb("gw", [P, NC, E])
        gw_hi, gw_lo = sb("gw_hi", [P, NC, E], F32R), sb("gw_lo", [P, NC, E], F32R)
        ebias = sb("ebias", [P, E])
        rope = sb("rope", [P, 2, T])
        stats, mv = sb("stats", [P, NT, 6]), sb("mv", [P, NT, 2])
        var, sd, rstd, tmp = (sb(n, [P, NT]) for n in ("var", "sd", "rstd", "tmp"))
        w_raw = sb("w_raw", [P, 2, C + 1])
        w_hi, w_lo = sb("w_hi", [P, 2, C], F32R), sb("w_lo", [P, 2, C], F32R)
        swapped = sb("swapped", [P, 2, TG])
        t1, t2 = sb("t1", [P, NG, TG]), sb("t2", [P, NG, TG])
        row_out = sb("row_out", [P, 4, C])
        inter_lo = sb("inter_lo", [P, NI, TG], F32R)
        zero_u = sb("zero_u", [P, E * CAP // P], U32)
        sel_b, before_b = sb("sel_b", [P, NT, E], BF16), sb("before_b", [P, NT, E], BF16)
        ones_b, upper_b = sb("ones_b", [P, P], BF16), sb("upper_b", [P, P], BF16)
        top = sb("top", [P, NT, 8])
        topi = sb("topi", [P, NT, 8], U32)
        topf = sb("topf", [P, NT, 8])
        wk, dk = sb("wk", [P, K, NT]), sb("dk", [P, K, NT])
        wsum, wrec = sb("wsum", [P, NT]), sb("wrec", [P, NT])
        scat = sb("scat", [P, K, NT], U32)
        tok = sb("tok", [P, NT], U32)
        cst = keep["cst"]
        sgu, sdn = xn[:, 0:4, :], xn[:, 4:6, :]
        route = lambda k: xn[:, 6 + k, :].rearrange("p (n e) -> p n e", e=E)
        hot = lambda k: route(k)
        logit, ra, rb, rc = (route(6 + k) for k in range(4))
        sgu_hi, sgu_lo = wv_hi, wv_lo
        sdn_hi, sdn_lo = w_hi, w_lo
        inter_hi = sb("inter_hi", [P, NI, TG], F32R)

        p_t = ctx.enter_context(nc.psum_tensor("p_t", [P, 2, 512], F32))
        p_p = ctx.enter_context(nc.psum_tensor("p_p", [P, 4, 512], F32))
        p_v = ctx.enter_context(nc.psum_tensor("p_v", [P, 2, 512], F32))
        ident = cst[:, C_ID:C_ID + P]
        p_pos = p_t[:, 0, :].rearrange("p (n e) -> p n e", e=E)

        x_loaded = [sem(f"x_loaded{q}") for q in range(NG)]
        const_loaded, small_loaded, wv_loaded, rope_loaded, tok_loaded = (
            sem(n) for n in ("const_loaded", "small_loaded", "wv_loaded", "rope_loaded", "tok_loaded"))
        var_ready, sd_ready, xn_ready, xn_stored = (sem(n) for n in ("var_ready", "sd_ready", "xn_ready", "xn_stored"))
        chain, parts_ready = sem("chain"), sem("parts_ready")
        wv_hi_ready, wv_ready = sem("wv_hi_ready"), sem("wv_ready")
        xt_psum, xt_hi_ready, xt_ready = sem("xt_psum"), sem("xt_hi_ready"), sem("xt_ready")
        logits_psum, logits_copied, logits_ready, v_psum, v_evicted = (
            sem(n) for n in ("logits_psum", "logits_copied", "logits_ready", "v_psum", "v_evicted"))
        row_stored = [sem(f"row_stored{k}") for k in range(4)]
        na_ready, exp_ready, lnin_ready, ln_ready, sp_ready, sqrt_ready = (
            sem(n) for n in ("na_ready", "exp_ready", "lnin_ready", "ln_ready", "sp_ready", "sqrt_ready"))
        sel_ready, pos_ready, route_ready = sem("sel_ready"), sem("pos_ready"), sem("route_ready")
        zero_ready, table_cleared, scattered = sem("zero_ready"), sem("table_cleared"), sem("scattered")
        w_loaded = [sem(f"w_loaded{b}") for b in range(2)]
        w_hi_ready, w_ready = sem("w_hi_ready"), sem("w_ready")
        qk_psum, swap_ready, t2_done, rot_ready = sem("qk_psum"), sem("swap_ready"), sem("t2_done"), sem("rot_ready")
        rot_stored = [sem(f"rot_stored{u}") for u in range(NG)]
        shared_loaded, shared_hi_ready, shared_ready = (
            sem("shared_loaded"), sem("shared_hi_ready"), sem("shared_ready"))
        gu_psum, silu_ready, gu_read, inter_ready = sem("gu_psum"), sem("silu_ready"), sem("gu_read"), sem("inter_ready")
        down_psum, down_evicted = sem("down_psum"), sem("down_evicted")
        block = ctx.enter_context(nc.Block())
        PAIRS = ROPED // 2
        FRONT, EARLY_V = [], 0
        for t in range(NT):
            FRONT.append(("transpose", t))
            if t % 4 == 3:
                if t + 1 < NT:
                    FRONT.append(("values", EARLY_V))
                    EARLY_V += 1
                FRONT.append(("logits", t // 4))
        xv = ins["x"].rearrange("(n p) c -> p n c", p=P)
        xnv = d["xn"].rearrange("(n p) c -> p n c", p=P)

        @block.sync
        def _(sp):
            sp.dma_start(cst[:, :], ins["cst"]).then_inc(const_loaded, 16)
            for q in range(NG):
                sp.dma_start(xn[:, 4 * q:4 * q + 4, :], xv[:, 4 * q:4 * q + 4, :]).then_inc(x_loaded[q], 16)
                if q == 0:
                    sp.dma_start(wv[:, :, :], ins["wv"]).then_inc(wv_loaded, 16)
            sp.dma_start(rope[:, :, :], ins["rope"]).then_inc(rope_loaded, 16)
            for b in range(2):
                sp.dma_start(w_raw[:, b, :], ins["wqk"][b]).then_inc(w_loaded[b], 16)
            for q in range(NG):
                sp.wait_ge(xn_ready, 4 * q + 4)
                sp.dma_start(xnv[:, 4 * q:4 * q + 4, :], xn[:, 4 * q:4 * q + 4, :]).then_inc(xn_stored, 16)
            sp.wait_ge(zero_ready, 1)
            sp.dma_start(d["slot_token"].rearrange("(p n) o -> p (n o)", p=P), zero_u[:, :]).then_inc(table_cleared, 16)
            for t in range(NT):
                sp.wait_ge(v_evicted, t + 1)
                sp.dma_start(d["v"][t * P:(t + 1) * P, :], row_out[:, t % 4, :]).then_inc(row_stored[t % 4], 16)
            sp.wait_ge(xn_stored, 16 * NG)
            sp.wait_ge(xt_psum, NT)
            sp.dma_start(sgu, ins["sgu"]).then_inc(shared_loaded, 16)
            sp.dma_start(sdn, ins["sdn"]).then_inc(shared_loaded, 16)
            for u in range(NG):
                sp.sem_inc(rot_stored[u], 16)

            def store(n):
                for u in range(NG):
                    sp.wait_ge(rot_ready, 4 * n + u + 1)
                    sp.dma_start(d["qk"][bass.ds(n, 1), :, u * TG:(u + 1) * TG], t1[:, u:u + 1, :])\
                      .then_inc(rot_stored[u], 16)
            with sp.Fori(0, PAIRS - 1) as i:
                for b in range(2):
                    store(2 * i + b)
                    sp.dma_start(w_raw[:, b:b + 1, :], ins["wqk"][bass.ds(2 * i + b + 2, 1)].rearrange("a p c -> p a c"))\
                      .then_inc(w_loaded[b], 16)
            store(ROPED - 2)
            store(ROPED - 1)
            for u in range(NG):
                sp.wait_ge(rot_stored[u], 16 * (ROPED + 1))
            for t in range(NT):
                sp.wait_ge(down_evicted, t + 1)
                sp.dma_start(d["shared"][t * P:(t + 1) * P, :], row_out[:, t % 4, :]).then_inc(row_stored[t % 4], 16)
            for k in range(4):
                sp.wait_ge(row_stored[k], 16 * 8)

        @block.gpsimd
        def _(pool):
            pool.memset(zero_u[:, :], 0).then_inc(zero_ready, 1)
            pool.wait_ge(const_loaded, 16)
            pool.wait_ge(wv_loaded, 16)
            nc.gpsimd.tensor_tensor(wv_hi.rearrange("p c (a b) -> p c a b", b=P), wv.rearrange("p c (a b) -> p c a b", b=P),
                                    cst[:, C_ONES:C_ONES + P].unsqueeze(1).unsqueeze(1).to_broadcast([P, NC, C // P, P]),
                                    ALU.mult).then_inc(wv_hi_ready, 1)
            pool.wait_ge(wv_hi_ready, 1)
            nc.gpsimd.tensor_tensor(wv_lo[:, :, :], wv[:, :, :], wv_hi[:, :, :].bitcast(F32), ALU.subtract).then_inc(wv_ready, 1)
            pool.wait_ge(tok_loaded, 16)
            pool.wait_ge(table_cleared, 16)
            pool.wait_ge(route_ready, 1)
            for t in range(NT):
                for k in range(K):
                    pool.indirect_dma_start(
                        d["slot_token"], bass.IndirectOffsetOnAxis(ap=scat[:, k, t:t + 1], axis=0),
                        tok[:, t:t + 1], None, bounds_check=E * CAP - 1, oob_is_err=False).then_inc(scattered, 16)
            pool.wait_ge(shared_loaded, 32)
            pool.wait_ge(v_psum, NT)
            ones = cst[:, C_ONES:C_ONES + P].unsqueeze(1).unsqueeze(1)
            blocks = lambda m: m.rearrange("p c (a b) -> p c a b", b=P)
            nc.gpsimd.tensor_tensor(blocks(sgu_hi), blocks(sgu), ones.to_broadcast([P, NC, C // P, P]), ALU.mult)\
              .then_inc(shared_hi_ready, 1)
            pool.wait_ge(shared_hi_ready, 1)
            nc.gpsimd.tensor_tensor(sgu_lo[:, :, :], sgu, sgu_hi[:, :, :].bitcast(F32), ALU.subtract).then_inc(shared_ready, 1)
            pool.wait_ge(qk_psum, 4 * ROPED)
            nc.gpsimd.tensor_tensor(blocks(sdn_hi), blocks(sdn), ones.to_broadcast([P, NI, C // P, P]), ALU.mult)\
              .then_inc(shared_hi_ready, 1)
            pool.wait_ge(shared_hi_ready, 2)
            nc.gpsimd.tensor_tensor(sdn_lo[:, :, :], sdn, sdn_hi[:, :, :].bitcast(F32), ALU.subtract).then_inc(shared_ready, 1)
            pool.wait_ge(scattered, 16 * NT * K)

        @block.scalar
        def _(act):
            act.dma_start(gw[:, :, :], ins["gate_w"]).then_inc(small_loaded, 16)
            act.dma_start(bv[:, :], ins["bv"]).then_inc(small_loaded, 16)
            act.dma_start(bo[:, :], ins["bo"]).then_inc(small_loaded, 16)
            act.dma_start(ebias[:, :], ins["ebias"].partition_broadcast(P)).then_inc(small_loaded, 16)
            act.dma_start(tok[:, :], ins["tok"]).then_inc(tok_loaded, 16)
            def deviation(q):
                act.wait_ge(var_ready, q + 1)
                nc.scalar.activation(sd[:, 4 * q:4 * q + 4], var[:, 4 * q:4 * q + 4], ACT.Sqrt).then_inc(sd_ready, 1)

            def transposed(t):
                act.wait_ge(xt_psum, t + 1)
                nc.scalar.activation(xt_hi[:, :, t * P:(t + 1) * P],
                                     p_t[:, t % 2, :].rearrange("p (c n) -> p c n", c=NC), ACT.Copy).then_inc(xt_hi_ready, 1)
                if t % 4 == 3 and t + 1 < NT:
                    deviation(t // 4 + 1)

            def logits(g):
                act.wait_ge(logits_psum, g + 1)
                nc.scalar.activation(t1[0:E, g, :], p_p[0:E, g, :], ACT.Copy).then_inc(logits_copied, 1)

            def value_rows(t):
                act.wait_ge(v_psum, t + 1)
                if t >= 4:
                    act.wait_ge(row_stored[t % 4], 16 * (t // 4))
                nc.scalar.activation(row_out[:, t % 4, :], p_v[:, t % 2, :], ACT.Copy).then_inc(v_evicted, 1)

            def weight_hi(b, count):
                act.wait_ge(w_loaded[b], 16 * count)
                nc.scalar.activation(w_hi[:, b, :], w_raw[:, b, 0:C], ACT.Copy).then_inc(w_hi_ready, 1)

            deviation(0)
            do = {"transpose": transposed, "logits": logits, "values": value_rows}
            for what, at in FRONT:
                do[what](at)
            weight_hi(0, 1)
            act.wait_ge(na_ready, 1)
            nc.scalar.activation(rb, ra, ACT.Exp).then_inc(exp_ready, 1)
            value_rows(EARLY_V)
            act.wait_ge(lnin_ready, 1)
            nc.scalar.activation(hot(1), rc, ACT.Ln).then_inc(ln_ready, 1)
            value_rows(EARLY_V + 1)
            act.wait_ge(sp_ready, 1)
            nc.scalar.activation(ra, rb, ACT.Sqrt).then_inc(sqrt_ready, 1)
            for t in range(EARLY_V + 2, NT):
                value_rows(t)
            def head(n, b, count):
                for u in range(NG):
                    act.wait_ge(qk_psum, 4 * n + u + 1)
                    act.wait_ge(t2_done, 4 * n + u + 3)
                    h = HD // 2
                    nc.scalar.activation(swapped[0:h, u % 2, :], p_p[h:P, u, :], ACT.Identity, bias=w_raw[h:P, b, C:C + 1])
                    nc.scalar.activation(swapped[h:P, u % 2, :], p_p[0:h, u, :], ACT.Identity, bias=w_raw[0:h, b, C:C + 1])\
                      .then_inc(swap_ready, 1)
                    if u == 1 and count is not None:
                        weight_hi(1 - b, count)
            with act.Fori(0, PAIRS - 1) as i:
                head(2 * i, 0, i + 1)
                head(2 * i + 1, 1, i + 2)
            head(ROPED - 2, 0, PAIRS)
            head(ROPED - 1, 1, None)
            def silu(g):
                for i in range(NI):
                    act.wait_ge(gu_psum, NI * g + i + 1)
                    if g:
                        act.wait_ge(inter_ready, NI * (g - 1) + i + 1)
                    nc.scalar.activation(t1[:, i, :], p_p[:, i, :], ACT.Silu).then_inc(silu_ready, 1)
            for u in range(NI):
                act.wait_ge(rot_stored[u], 16 * (ROPED + 1))
            silu(0)
            for g in range(NG):
                if g + 1 < NG:
                    silu(g + 1)
                for r in range(4):
                    t = 4 * g + r
                    act.wait_ge(down_psum, t + 1)
                    act.wait_ge(row_stored[t % 4], 16 * (4 + t // 4))
                    nc.scalar.activation(row_out[:, t % 4, :], p_v[:, t % 2, :], ACT.Copy).then_inc(down_evicted, 1)

        @block.vector
        def _(dve):
            v = nc.vector
            steps = [0]

            def link(instruction):
                steps[0] += 1
                instruction.then_inc(chain, 1)
                dve.wait_ge(chain, steps[0])

            def publish(instruction, semaphore):
                instruction.then_inc(semaphore, 1)
                dve.wait_ge(semaphore, 1)

            def weight_lo(b, count):
                dve.wait_ge(w_hi_ready, count)
                v.tensor_tensor(w_lo[:, b, :], w_raw[:, b, 0:C], w_hi[:, b, :].bitcast(F32), ALU.subtract).then_inc(w_ready, 1)

            for q in range(NG):
                dve.wait_ge(x_loaded[q], 16)
                s = slice(4 * q, 4 * q + 4)
                for t in range(4 * q, 4 * q + 4):
                    last = v.bn_stats(stats[:, t, :], xn[:, t, :])
                link(last)
                for t in range(4 * q, 4 * q + 4):
                    last = v.bn_aggr(mv[:, t, :], stats[:, t, :])
                link(last)
                v.tensor_scalar(var[:, s], mv[:, s, 1], EPS, None, ALU.add).then_inc(var_ready, 1)
                dve.wait_ge(sd_ready, q + 1)
                link(v.reciprocal(rstd[:, s], sd[:, s]))
                link(v.tensor_tensor(tmp[:, s], rstd[:, s], rstd[:, s], ALU.mult))
                link(v.tensor_tensor(tmp[:, s], tmp[:, s], var[:, s], ALU.mult))
                link(v.tensor_scalar(tmp[:, s], tmp[:, s], -0.5, 1.5, ALU.mult, ALU.add))
                link(v.tensor_tensor(rstd[:, s], rstd[:, s], tmp[:, s], ALU.mult))
                for t in range(4 * q, 4 * q + 4):
                    v.tensor_scalar(xn[:, t, :], xn[:, t, :], mv[:, t, 0:1], rstd[:, t:t + 1],
                                    ALU.subtract, ALU.mult).then_inc(xn_ready, 1)
                for t in range(4 * q, 4 * q + 4):
                    dve.wait_ge(xt_hi_ready, t + 1)
                    col = slice(t * P, (t + 1) * P)
                    v.tensor_tensor(xt_lo[:, :, col], p_t[:, t % 2, :].rearrange("p (c n) -> p c n", c=NC),
                                    xt_hi[:, :, col].bitcast(F32), ALU.subtract).then_inc(xt_ready, 1)
                if q == 0:
                    dve.wait_ge(const_loaded, 16)
                    dve.wait_ge(small_loaded, 64)
                    v.tensor_copy(ones_b[:, :], cst[:, C_ONES:C_ONES + P])
                    v.tensor_copy(upper_b[:, :], cst[:, C_UPPER:C_UPPER + P])
                    v.tensor_copy(one_r[:, :], cst[0:1, C_ONES:C_ONES + P])
                    v.tensor_copy(gw_hi[:, :, :], gw[:, :, :])
                    v.tensor_copy(keep["bo_hi"][:, :], bo[:, :])
                    link(v.tensor_copy(bv_hi[:, :], bv[:, :]))
                    v.tensor_tensor(gw_lo[:, :, :], gw[:, :, :], gw_hi[:, :, :].bitcast(F32), ALU.subtract)
                    v.tensor_tensor(bv_lo[:, :], bv[:, :], bv_hi[:, :].bitcast(F32), ALU.subtract)
                    v.tensor_tensor(keep["bo_lo"][:, :], bo[:, :], keep["bo_hi"][:, :].bitcast(F32), ALU.subtract).then_inc(parts_ready, 1)
            dve.sem_inc(t2_done, 4)
            weight_lo(0, 1)
            dve.wait_ge(logits_ready, 1)
            dve.wait_ge(xn_stored, 16 * NG)
            link(v.tensor_copy(logit, p_pos))
            v.scalar_tensor_tensor(ra, logit, -1.0, logit, ALU.mult, ALU.min).then_inc(na_ready, 1)
            dve.wait_ge(exp_ready, 1)
            publish(v.tensor_scalar(rc, rb, 1.0, None, ALU.add), lnin_ready)
            link(v.scalar_tensor_tensor(ra, rc, -1.0, rb, ALU.add, ALU.subtract))
            link(v.reciprocal(hot(0), rc))
            link(v.scalar_tensor_tensor(ra, ra, -1.0, hot(0), ALU.mult, ALU.mult))
            link(v.scalar_tensor_tensor(ra, logit, 0.0, ra, ALU.max, ALU.add))
            dve.wait_ge(ln_ready, 1)
            v.scalar_tensor_tensor(rb, hot(1), 2e-35, ra, ALU.max, ALU.add).then_inc(sp_ready, 1)
            dve.wait_ge(sqrt_ready, 1)
            link(v.reciprocal(rc, ra))
            link(v.tensor_tensor(rc, rc, rb, ALU.mult))
            link(v.tensor_tensor(ra, ra, rc, ALU.add))
            link(v.tensor_scalar(ra, ra, 0.5, None, ALU.mult))
            score = ra
            link(v.tensor_tensor(rb, score, ebias[:, :].unsqueeze(1).to_broadcast([P, NT, E]), ALU.add))
            for t in range(NT):
                last = v.max(top[:, t, :], rb[:, t, :])
            link(last)
            for t in range(NT):
                last = v.max_index(topi[:, t, :], top[:, t, :], rb[:, t, :])
            link(last)
            link(v.tensor_copy(topf[:, :, :], topi[:, :, :]))
            item = cst[:, C_ITEM:C_ITEM + E].unsqueeze(1).to_broadcast([P, NT, E])
            for k in range(K):
                last = v.tensor_tensor(hot(k), item, topf[:, :, k:k + 1].to_broadcast([P, NT, E]), ALU.is_equal)
            link(last)
            link(v.tensor_tensor(rc, hot(0), hot(1), ALU.add))
            for k in range(2, K - 1):
                link(v.tensor_tensor(rc, rc, hot(k), ALU.add))
            link(v.tensor_tensor(sel_b[:, :, :], rc, hot(K - 1), ALU.add))
            v.memset(before_b[:, 0, :], 0.0)
            link(v.tensor_copy(before_b[:, 1, :], sel_b[:, 0, :]))
            for t in range(2, NT - 1):
                link(v.tensor_tensor(before_b[:, t, :], before_b[:, t - 1, :], sel_b[:, t - 1, :], ALU.add))
            v.tensor_tensor(before_b[:, NT - 1, :], before_b[:, NT - 2, :], sel_b[:, NT - 2, :], ALU.add).then_inc(sel_ready, 1)
            dve.wait_ge(pos_ready, 1)
            link(v.tensor_scalar(rb, p_pos, float(CAP), FAR, ALU.is_ge, ALU.mult))
            link(v.tensor_tensor(rb, p_pos, rb, ALU.add))
            link(v.tensor_tensor(rb, rb, cst[:, C_BASE:C_BASE + E].unsqueeze(1).to_broadcast([P, NT, E]), ALU.add))
            for k in range(K):
                link(v.tensor_tensor(rc, hot(k), rb, ALU.mult))
                link(v.tensor_reduce(dk[:, k, :], rc, AX.X, ALU.add))
            v.tensor_copy(scat[:, :, :], dk[:, :, :]).then_inc(route_ready, 1)
            def rotate(n, u, scale):
                dve.wait_ge(t2_done, 4 * n + u + 5)
                v.scalar_tensor_tensor(t1[:, u, :], t1[:, u, :], scale, t2[:, u, :],
                                       ALU.mult, ALU.add).then_inc(rot_ready, 1)

            def head(n, b, scale, more):
                for u in range(NG):
                    cols = slice(u * TG, (u + 1) * TG)
                    dve.wait_ge(rot_stored[u], 16 * n + 16)
                    dve.wait_ge(swap_ready, 4 * n + u + 1)
                    v.scalar_tensor_tensor(t1[:, u, :], p_p[:, u, :], w_raw[:, b, C:C + 1], rope[:, 0, cols],
                                           ALU.add, ALU.mult)
                    v.scalar_tensor_tensor(t2[:, u, :], swapped[:, u % 2, :], scale, rope[:, 1, cols],
                                           ALU.mult, ALU.mult).then_inc(t2_done, 1)
                    if u:
                        rotate(n, u - 1, scale)
                    if u == 1 and more:
                        weight_lo(1 - b, n + 2)
                rotate(n, NG - 1, scale)
            dve.wait_ge(rope_loaded, 16)
            with dve.Fori(0, HEADS // 2) as i:
                head(2 * i, 0, QSCALE, True)
                head(2 * i + 1, 1, QSCALE, True)
            with dve.Fori(HEADS // 2, PAIRS - 1) as i:
                head(2 * i, 0, 1.0, True)
                head(2 * i + 1, 1, 1.0, True)
            head(ROPED - 2, 0, 1.0, True)
            head(ROPED - 1, 1, 1.0, False)
            for g in range(NG):
                for i in range(NI):
                    dve.wait_ge(silu_ready, NI * g + i + 1)
                    link(v.tensor_tensor(t1[:, i, :], t1[:, i, :], p_p[:, 2 + i, :], ALU.mult))
                    v.tensor_scalar(t1[:, i, :], t1[:, i, :], CLIP, -CLIP, ALU.min, ALU.max).then_inc(gu_read, 1)
                    dve.wait_ge(gu_read, NI * g + i + 1)
                    if g:
                        dve.wait_ge(down_psum, 4 * g)
                    link(v.tensor_copy(inter_hi[:, i, :], t1[:, i, :]))
                    v.tensor_tensor(inter_lo[:, i, :], t1[:, i, :], inter_hi[:, i, :].bitcast(F32),
                                    ALU.subtract).then_inc(inter_ready, 1)
                if g < K // 2:
                    for k in (2 * g, 2 * g + 1):
                        link(v.tensor_tensor(rc, hot(k), score, ALU.mult))
                        link(v.tensor_reduce(wk[:, k, :], rc, AX.X, ALU.add))
            link(v.tensor_tensor(wsum[:, :], wk[:, 0, :], wk[:, 1, :], ALU.add))
            for k in range(2, K):
                link(v.tensor_tensor(wsum[:, :], wsum[:, :], wk[:, k, :], ALU.add))
            link(v.reciprocal(wrec[:, :], wsum[:, :]))
            held = rb.rearrange("p n e -> p (n e)")[:, 0:K * NT].rearrange("p (k n) -> p k n", k=K)
            link(v.tensor_scalar(held, dk[:, :, :], FAR, None, ALU.is_lt))
            link(v.tensor_tensor(wk[:, :, :], wk[:, :, :], held, ALU.mult))
            for k in range(K):
                v.scalar_tensor_tensor(keep["weight"][:, k, :], wk[:, k, :], ROUTE_SCALE, wrec[:, :], ALU.mult, ALU.mult)
            link(v.tensor_tensor(dk[:, :, :], dk[:, :, :], held, ALU.mult))
            link(v.tensor_copy(keep["slot"][:, :, :], dk[:, :, :]))

        @block.tensor
        def _(pe):
            pe.wait_ge(const_loaded, 16)
            def transposes(t):
                pe.wait_ge(xn_ready, t + 1)
                if t >= 2:
                    pe.wait_ge(xt_ready, t - 1)
                for c in range(NC):
                    last = nc.tensor.transpose(p_t[:, t % 2, c * P:(c + 1) * P], xn[:, t, c * P:(c + 1) * P], ident)
                last.then_inc(xt_psum, 1)

            def logits(g):
                pe.wait_ge(xt_ready, 4 * g + 4)
                for c in range(NC):
                    cols = slice(g * TG, (g + 1) * TG)
                    last = three_passes(nc, p_p[0:E, g, :], gw_hi[:, c, :], gw_lo[:, c, :],
                                        xt_hi[:, c, cols], xt_lo[:, c, cols], c == 0, c == NC - 1)
                last.then_inc(logits_psum, 1)

            def values(t):
                a = slice(t * P, (t + 1) * P)
                pe.wait_ge(xt_ready, t + 1)
                if t == 0:
                    pe.wait_ge(wv_ready, 1)
                    pe.wait_ge(parts_ready, 1)
                if t >= 2:
                    pe.wait_ge(v_evicted, t - 1)
                out = p_v[:, t % 2, :]
                for c in range(NC):
                    three_passes(nc, out, xt_hi[:, c, a], xt_lo[:, c, a], wv_hi[:, c, :], wv_lo[:, c, :], c == 0, False)
                nc.tensor.matmul(out, one_r[:, :], bv_hi[:, :], start=False, stop=False)
                nc.tensor.matmul(out, one_r[:, :], bv_lo[:, :], start=False, stop=True).then_inc(v_psum, 1)

            do = {"transpose": transposes, "logits": logits, "values": values}
            for what, at in FRONT:
                do[what](at)
            pe.wait_ge(logits_copied, NG)
            for t in range(NT):
                last = nc.tensor.transpose(p_pos[:, t, :], t1[0:E, t // 4, t % 4 * P:(t % 4 + 1) * P],
                                           cst[0:E, C_ID:C_ID + E])
            last.then_inc(logits_ready, 1)
            def positions():
                pe.wait_ge(sel_ready, 1)
                nc.tensor.matmul(p_t[:, 0, :], upper_b[:, :], sel_b[:, :, :], start=True, stop=False)
                nc.tensor.matmul(p_t[:, 0, :], ones_b[:, :], before_b[:, :, :], start=False, stop=True).then_inc(pos_ready, 1)

            for t in range(EARLY_V, NT):
                values(t)
                if t == NT - 3:
                    positions()

            def head(n, b):
                pe.wait_ge(w_ready, n + 1)
                for u in range(NG):
                    cols = slice(u * TG, (u + 1) * TG)
                    pe.wait_ge(t2_done, 4 * n + u + 1)
                    for c in range(NC):
                        w = slice(c * HD, (c + 1) * HD)
                        last = three_passes(nc, p_p[:, u, :], w_hi[:, b, w], w_lo[:, b, w],
                                            xt_hi[:, c, cols], xt_lo[:, c, cols], c == 0, c == NC - 1)
                    last.then_inc(qk_psum, 1)
            with pe.Fori(0, PAIRS) as i:
                head(2 * i, 0)
                head(2 * i + 1, 1)
            pe.wait_ge(shared_ready, 1)

            def gate_up(g):
                cols = slice(g * TG, (g + 1) * TG)
                for i in range(NI):
                    if g == 0:
                        pe.wait_ge(t2_done, 4 * ROPED + NI + i + 1)
                    else:
                        pe.wait_ge(gu_read, NI * (g - 1) + i + 1)
                    for k in (i, NI + i):
                        for c in range(NC):
                            w = slice(k * P, (k + 1) * P)
                            last = three_passes(nc, p_p[:, k, :], sgu_hi[:, c, w], sgu_lo[:, c, w],
                                                xt_hi[:, c, cols], xt_lo[:, c, cols], c == 0, c == NC - 1)
                    last.then_inc(gu_psum, 1)
            gate_up(0)
            for g in range(NG):
                if g + 1 < NG:
                    gate_up(g + 1)
                pe.wait_ge(shared_ready, 2)
                pe.wait_ge(inter_ready, NI * (g + 1))
                for r in range(4):
                    t = 4 * g + r
                    if t >= 2:
                        pe.wait_ge(down_evicted, t - 1)
                    for i in range(NI):
                        a = slice(r * P, (r + 1) * P)
                        last = three_passes(nc, p_v[:, t % 2, :], inter_hi[:, i, a], inter_lo[:, i, a],
                                            sdn_hi[:, i, :], sdn_lo[:, i, :], i == 0, i == NI - 1)
                    last.then_inc(down_psum, 1)


def attend(nc, ins, d, keep):
    UNITS = [4 * (r + 1) for r in range(NG)]
    BEFORE = [sum(UNITS[:r]) for r in range(NG)]
    HU = sum(UNITS)
    JU = G * HU
    SRING, TRING, PRING, NRING = 5, 2, 4, 8
    LAG = 2
    EXP_LAG = 4
    AHEAD = 4 * NG + EXP_LAG + 2
    HOLD = 4
    EXTRA = [4 * a + 3 for a in range(HOLD)]
    with ExitStack() as ctx:
        sb = lambda n, s, dt=F32: ctx.enter_context(nc.sbuf_tensor(n, s, dt))
        ps = lambda n, s: ctx.enter_context(nc.psum_tensor(n, s, F32))
        sem = lambda n: ctx.enter_context(nc.semaphore(n))
        q_raw, k_raw = (keep["pair_raw"][:, b, :].rearrange("p (r n) -> p r n", r=NG) for b in range(2))
        v_raw = keep["rows_raw"][:, :].rearrange("p (n c) -> p n c", c=HD)
        gu_raw = keep["pair_raw"][:, :, :].rearrange("p b (c n) -> p b c n", c=NC)
        token_rows = keep["rows_raw"][0:HALF, :].rearrange("p (b h c) -> p b h c", b=2, h=2)
        q_hi, q_lo = sb("q_hi", [P, T], F32R), sb("q_lo", [P, T], F32R)
        k_hi, k_lo = sb("k_hi", [P, T], F32R), sb("k_lo", [P, T], F32R)
        v_hi, v_lo = sb("v_hi", [P, NT, HD], F32R), sb("v_lo", [P, NT, HD], F32R)
        prob = sb("prob", [P, HU, TG])
        pt_hi, pt_lo = sb("pt_hi", [P, PRING, TG], F32R), sb("pt_lo", [P, PRING, TG], F32R)
        chunk_max, neg_max = sb("chunk_max", [P, NRING, 4]), sb("neg_max", [P, NRING])
        chunk_sum, row_sum = sb("chunk_sum", [P, NG, 4, NG]), sb("row_sum", [P, NG, 4])
        inv_sum = sb("inv_sum", [P, NG, 4])
        inv_cols = sb("inv_cols", [P, 2, TG])
        head_out = sb("head_out", [P, 2, TG])
        ident_b, mask_b = sb("ident_b", [P, P], BF16), sb("mask_b", [P, P], BF16)
        cst = keep["cst"]
        ident, ones = cst[:, C_ID:C_ID + P], cst[:, C_ONES:C_ONES + P]
        p_s, p_t, p_o = ps("p_s", [P, SRING, 512]), ps("p_tr", [P, TRING, 512]), ps("p_o", [P, 512])

        const_ready = sem("const_ready")
        q_loaded = [sem(f"q_loaded{r}") for r in range(NG)]
        k_loaded = [sem(f"k_loaded{r}") for r in range(NG)]
        v_loaded = [sem(f"v_loaded{r}") for r in range(NG)]
        split_hi = sem("split_hi")
        q_split, k_split, v_split = sem("q_split"), sem("k_split"), sem("v_split")
        scores_ready, max_chain, max_ready, exp_done = sem("scores_ready"), sem("max_chain"), sem("max_ready"), sem("exp_done")
        bank_filled, pt_hi_ready, pt_ready = sem("bank_filled"), sem("pt_hi_ready"), sem("pt_ready")
        sum_chain, inv_ready, inv_stored = sem("sum_chain"), sem("inv_ready"), sem("inv_stored")
        cols_loaded = [sem(f"cols_loaded{b}") for b in range(2)]
        pv_done, out_ready = sem("pv_done"), sem("out_ready")
        index_loaded, weights_loaded, rows_gathered = (
            sem(n) for n in ("first_index_loaded", "first_weights_loaded", "first_rows_gathered"))
        out_stored = [sem(f"out_stored{b}") for b in range(2)]
        SCORE_CREDIT, PV_CREDIT = HU, 16
        block = ctx.enter_context(nc.Block())
        groups = [(g, r) for g in range(G) for r in range(NG)]

        def rows(g, r):
            return [(i, 16 * g + 4 * r + i, r + 1) for i in range(4)]

        def chunk_index(g, r, i, c):
            return HU * g + BEFORE[r] + i * (r + 1) + c

        def width(r, i, c):
            return TG if c < r else P * (i + 1)

        def unit_index(g, r, k):
            return HU * g + BEFORE[r] + k

        def first_row(r, k):
            return max(0, k - 4 * r)

        chunks = [(g, r, i, c) for g in range(G + 1) for r in range(NG) for i in range(4) for c in range(r + 1)]
        opening = [("chunk", *c) for c in chunks[:AHEAD - HOLD]]

        def turns(more):
            made = AHEAD - HOLD
            for u, (g, r, k) in enumerate((g, r, k) for g, r in groups for k in range(UNITS[r])):
                if k == LAG - 1 and (g, r) != groups[0]:
                    yield "out", *groups[NG * g + r - 1], 0
                yield "unit", g, r, k
                want = u + 1 + AHEAD - HOLD + sum(u >= a for a in EXTRA)
                want = min(want, JU) if u + 1 + AHEAD - HOLD < JU else u + 1 + AHEAD - HOLD
                for c in chunks[made:want] if more or made < JU else []:
                    yield "chunk", *c
                made = max(made, want)
            yield "out", *groups[-1], 0

        def late_chunks():
            return chunks[AHEAD - HOLD - EXP_LAG:AHEAD - HOLD]

        def for_each_head(engine, do):
            with engine.Fori(0, KV - 1) as j:
                do(j, True)
            do(KV - 1, False)

        @block.sync
        def _(sp):
            def load(j, g, r):
                if g == 0:
                    sp.wait_ge(k_split, 4 * j + r + 1)
                    sp.dma_start(k_raw[:, r:r + 1, :], d["qk"][bass.ds(HEADS + j, 1), :, r * TG:(r + 1) * TG]
                                 .rearrange("a p n -> p a n")).then_inc(k_loaded[r], 16)
                sp.wait_ge(q_split, 16 * j + 4 * g + r + 1)
                sp.dma_start(q_raw[:, r:r + 1, :], d["qk"][bass.ds(G * j + g, 1), :, r * TG:(r + 1) * TG]
                             .rearrange("a p n -> p a n")).then_inc(q_loaded[r], 16)
                if g == 0:
                    sp.wait_ge(v_split, 4 * j + r + 1)
                    sp.dma_start(v_raw[:, 4 * r:4 * r + 4, :],
                                 d["v"].rearrange("(n p) c -> p n c", p=P)[:, 4 * r:4 * r + 4, bass.ds(j * HD, HD)])\
                      .then_inc(v_loaded[r], 16)

            with sp.Fori(0, KV) as j:
                for r in range(NG):
                    load(j, 0, r)
                for g, r in groups[NG:]:
                    load(j, g, r)
            for e in range(2):
                for h in range(2):
                    sp.dma_start(keep["index"][:, e, h:h + 1], d["slot_token"][e * CAP + h * HALF:e * CAP + (h + 1) * HALF, :])\
                      .then_inc(index_loaded, 16)
            sp.wait_ge(q_split, 16 * KV + 4)
            sp.wait_ge(k_split, 4 * KV + 4)
            for e in range(2):
                sp.dma_start(gu_raw[:, e, :, :], ins["wgu"][e]).then_inc(weights_loaded, 16)
            sp.wait_ge(weights_loaded, 32)

        @block.gpsimd
        def _(pool):
            def split(hi, lo, raw, done, count):
                blocks = lambda m: m.rearrange("p (a b) -> p a b", b=P) if len(m.shape) == 2 else m
                nc.gpsimd.tensor_tensor(blocks(hi), blocks(raw), ones.unsqueeze(1).to_broadcast([P, TG // P, P]),
                                        ALU.mult).then_inc(split_hi, 1)
                pool.wait_ge(split_hi, count)
                nc.gpsimd.tensor_tensor(lo, raw, hi.bitcast(F32), ALU.subtract).then_inc(done, 1)

            for s in (q_split, k_split, v_split):
                pool.sem_inc(s, 4)
            with pool.Fori(0, KV) as j:
                at = [0]

                def nth():
                    at[0] += 1
                    return 24 * j + at[0]

                def queries(g, r):
                    cols = slice(r * TG, (r + 1) * TG)
                    pool.wait_ge(q_loaded[r], 64 * j + 16 * g + 16)
                    pool.wait_ge(scores_ready, JU * j + HU * g - HU + BEFORE[r] + UNITS[r] + SCORE_CREDIT)
                    split(q_hi[:, cols], q_lo[:, cols], q_raw[:, r, :], q_split, nth())

                def keys(r):
                    cols = slice(r * TG, (r + 1) * TG)
                    pool.wait_ge(k_loaded[r], 16 * j + 16)
                    pool.wait_ge(scores_ready, JU * j + SCORE_CREDIT)
                    split(k_hi[:, cols], k_lo[:, cols], k_raw[:, r, :], k_split, nth())

                def values(r):
                    pool.wait_ge(v_loaded[r], 16 * j + 16)
                    pool.wait_ge(pv_done, JU * j - UNITS[NG - 1] + 4 * r + 4 + PV_CREDIT)
                    split(v_hi[:, 4 * r:4 * r + 4, :], v_lo[:, 4 * r:4 * r + 4, :],
                          v_raw[:, 4 * r:4 * r + 4, :], v_split, nth())

                queries(0, 0)
                keys(0)
                queries(0, 1)
                keys(1)
                for r in range(2, NG):
                    keys(r)
                    queries(0, r)
                for g, r in groups[NG:]:
                    queries(g, r)
                    if g == 1:
                        values(r)
            pool.wait_ge(v_split, 4 * KV + 4)
            pool.wait_ge(index_loaded, 64)
            for e in range(2):
                for h in range(2):
                    pool.indirect_dma_start(token_rows[:, e, h, :], None, d["xn"],
                                            bass.IndirectOffsetOnAxis(ap=keep["index"][:, e, h:h + 1], axis=0),
                                            bounds_check=T - 1, oob_is_err=False).then_inc(rows_gathered, 16)
            pool.wait_ge(rows_gathered, 64)

        @block.scalar
        def _(act):
            act.sem_inc(exp_done, SRING)
            act.sem_inc(inv_stored, 16 * NG)
            for b in range(2):
                act.sem_inc(out_stored[b], 16)

            def head(j, more, begin=False):
                late = [] if begin else late_chunks()

                def exp(g, r, i, c):
                    row, m, w = 16 * g + 4 * r + i, chunk_index(g, r, i, c), width(r, i, c)
                    if c == 0:
                        act.wait_ge(max_ready, 64 * j + row + 1)
                    nc.scalar.activation(prob[:, m % HU, 0:w], p_s[:, m % SRING, 0:w], ACT.Exp,
                                         bias=neg_max[:, row % NRING:row % NRING + 1],
                                         accum_out=chunk_sum[:, r, i, c:c + 1]).then_inc(exp_done, 1)

                def chunk(g, r, i, c):
                    late.append((g, r, i, c))
                    if len(late) > EXP_LAG:
                        exp(*late.pop(0))

                def unit(g, r, k):
                    m, x, n = unit_index(g, r, k), P * first_row(r, k), NG * g + r
                    act.wait_ge(bank_filled, JU * j + m + 1)
                    act.wait_ge(pv_done, JU * j + m - PRING + 1 + PV_CREDIT)
                    nc.scalar.activation(pt_hi[:, m % PRING, x:TG], p_t[:, m % TRING, x:TG], ACT.Copy)\
                      .then_inc(pt_hi_ready, 1)
                    if late and m + AHEAD >= JU and not (more and m + AHEAD - HOLD >= JU):
                        exp(*late.pop(0))
                    if k == 1:
                        spread_sums(n)
                    if k == LAG and n:
                        store(n - 1)
                    if k == min(4, UNITS[r] - 1):
                        fetch_sums(n)

                def spread_sums(n):
                    g, r = groups[n]
                    act.wait_ge(inv_ready, 16 * j + n + 1)
                    nc.scalar.dma_start(d["inv"][bass.ds(16 * j + n, 1), :].rearrange("a (p i) -> p (a i)", i=4),
                                        inv_sum[:, r, :]).then_inc(inv_stored, 16)

                def fetch_sums(n):
                    act.wait_ge(inv_stored, 16 * (16 * j + n + 1 + NG))
                    act.wait_ge(out_ready, 16 * j + n + 1)
                    nc.scalar.dma_start(inv_cols[:, n % 2, :], d["inv"][bass.ds(16 * j + n, 1), :]
                                        .rearrange("a n -> (a n)").partition_broadcast(P)).then_inc(cols_loaded[n % 2], 16)

                def store(n):
                    g, r = groups[n]
                    act.wait_ge(out_ready, 16 * j + n + 1 + 2)
                    nc.scalar.dma_start(d["o"][bass.ds(KV * g + j, 1), :, r * TG:(r + 1) * TG].rearrange("a p n -> p a n"),
                                        head_out[:, n % 2:n % 2 + 1, :]).then_inc(out_stored[n % 2], 16)

                do = {"chunk": chunk, "unit": unit, "out": lambda *_: None}
                for what, *at in opening if begin else turns(more):
                    do[what](*at)
                if not begin:
                    store(len(groups) - 1)

            head(0, True, begin=True)
            for_each_head(act, head)
            for b in range(2):
                act.wait_ge(out_stored[b], 16 + 16 * KV * len(groups) // 2)

        @block.vector
        def _(dve):
            v = nc.vector
            v.tensor_copy(mask_b[:, :], cst[:, C_MASK:C_MASK + P]).then_inc(const_ready, 1)
            v.tensor_copy(ident_b[:, :], ident).then_inc(const_ready, 1)
            dve.sem_inc(out_ready, 2)
            dve.sem_inc(pt_ready, TRING)

            def head(j, more, begin=False):
                def chunk(g, r, i, c):
                    m, row = chunk_index(g, r, i, c), 16 * g + 4 * r + i
                    dve.wait_ge(scores_ready, JU * j + m + 1 + SCORE_CREDIT)
                    s = p_s[:, m % SRING, 0:width(r, i, c)]
                    nm = neg_max[:, row % NRING:row % NRING + 1]
                    if r == 0:
                        v.tensor_reduce(nm, s, AX.X, ALU.max, negate=True).then_inc(max_ready, 1)
                        return
                    v.tensor_reduce(chunk_max[:, row % NRING, c:c + 1], s, AX.X, ALU.max).then_inc(max_chain, 1)
                    if c == r:
                        made = (HU - UNITS[0]) * (4 * j + g) + BEFORE[r] - UNITS[0] + (i + 1) * (r + 1)
                        dve.wait_ge(max_chain, made)
                        v.tensor_reduce(nm, chunk_max[:, row % NRING, 0:r + 1], AX.X, ALU.max, negate=True).then_inc(max_ready, 1)

                def unit(g, r, k):
                    m, x = unit_index(g, r, k), P * first_row(r, k)
                    if k == 0:
                        inverse(g, r)
                    dve.wait_ge(pt_hi_ready, JU * j + m + 1)
                    v.tensor_tensor(pt_lo[:, m % PRING, x:TG], p_t[:, m % TRING, x:TG],
                                    pt_hi[:, m % PRING, x:TG].bitcast(F32), ALU.subtract).then_inc(pt_ready, 1)

                def inverse(g, r):
                    n = 4 * g + r
                    dve.wait_ge(exp_done, JU * j + BEFORE[r] + HU * g + UNITS[r] + SRING)
                    v.tensor_reduce(row_sum[:, r, :], chunk_sum[:, r, :, 0:r + 1], AX.X, ALU.add).then_inc(sum_chain, 1)
                    dve.wait_ge(sum_chain, 16 * j + n + 1)
                    dve.wait_ge(inv_stored, 16 * (16 * j + n + 1))
                    v.reciprocal(inv_sum[:, r, :], row_sum[:, r, :]).then_inc(inv_ready, 1)

                def out(g, r, _):
                    n = 4 * g + r
                    dve.wait_ge(cols_loaded[n % 2], 16 * (8 * j + n // 2 + 1))
                    dve.wait_ge(pv_done, JU * j + unit_index(g, r, UNITS[r] - 1) + 1 + PV_CREDIT)
                    dve.wait_ge(out_stored[n % 2], 16 * (8 * j + n // 2) + 16)
                    v.tensor_tensor(head_out[:, n % 2, :].rearrange("p (i q) -> p i q", i=4), p_o.rearrange("p (i q) -> p i q", i=4),
                                    inv_cols[:, n % 2, :].rearrange("p (q i) -> p i q", i=4), ALU.mult).then_inc(out_ready, 1)

                do = {"chunk": chunk, "unit": unit, "out": out}
                for what, *at in opening if begin else turns(more):
                    do[what](*at)

            head(0, True, begin=True)
            for_each_head(dve, head)

        @block.tensor
        def _(pe):
            pe.wait_ge(const_ready, 2)
            pe.sem_inc(scores_ready, SCORE_CREDIT)
            pe.sem_inc(pv_done, PV_CREDIT)

            def head(j, more, begin=False):
                waiting = []

                def chunk(g, r, i, c):
                    m, w = chunk_index(g, r, i, c), width(r, i, c)
                    if i == 0 and c == 0:
                        pe.wait_ge(q_split, 16 * j + 4 * g + r + 1 + 4)
                        if g % G == 0:
                            pe.wait_ge(k_split, 4 * j + g + r + 1 + 4)
                    pe.wait_ge(exp_done, JU * j + m + 1)
                    a, keys = slice((4 * r + i) * P, (4 * r + i + 1) * P), slice(c * TG, c * TG + w)
                    out = p_s[:, m % SRING, 0:w]
                    nc.tensor.matmul(out, q_hi[:, a], k_hi[:, keys], start=True, stop=False)
                    if c == r:
                        nc.tensor.matmul(p_s[:, m % SRING, w - P:w], ident_b[:, :], mask_b[:, :], start=False, stop=False)
                    nc.tensor.matmul(out, q_hi[:, a], k_lo[:, keys], start=False, stop=False)
                    nc.tensor.matmul(out, q_lo[:, a], k_hi[:, keys], start=False, stop=True).then_inc(scores_ready, 1)

                def multiply(g, r, k):
                    m, x = unit_index(g, r, k), P * first_row(r, k)
                    if g == 0 and k % 4 == 0 and k // 4 == r:
                        pe.wait_ge(v_split, 4 * j + r + 1 + 4)
                    if k == 0:
                        pe.wait_ge(out_ready, 16 * j + 4 * g + r + 2)
                    pe.wait_ge(pt_ready, JU * j + m + 1 + TRING)
                    last = three_passes(nc, p_o[:, x:TG], v_hi[:, k, :], v_lo[:, k, :],
                                        pt_hi[:, m % PRING, x:TG], pt_lo[:, m % PRING, x:TG], k == 0, k == UNITS[r] - 1)
                    last.then_inc(pv_done, 1)

                def unit(g, r, k):
                    m = unit_index(g, r, k)
                    pe.wait_ge(pt_ready, JU * j + m + 1)
                    for i in range(first_row(r, k), 4):
                        if k == 0:
                            pe.wait_ge(exp_done, JU * j + chunk_index(g, r, i, r) + 1 + SRING)
                        last = nc.tensor.transpose(p_t[:, m % TRING, i * P:(i + 1) * P],
                                                   prob[:, chunk_index(0, r, i, k // 4), k % 4 * P:(k % 4 + 1) * P], ident)
                    last.then_inc(bank_filled, 1)
                    waiting.append((g, r, k))
                    if len(waiting) > LAG:
                        multiply(*waiting.pop(0))

                do = {"chunk": chunk, "unit": unit, "out": lambda *_: None}
                for what, *at in opening if begin else turns(more):
                    do[what](*at)
                while waiting:
                    multiply(*waiting.pop(0))

            head(0, True, begin=True)
            for_each_head(pe, head)


def turn(nc, tick, source, turned, n):
    nc.gpsimd.wait_ge(turned, n + 1)
    nc.gpsimd.tensor_tensor(tick[:, :], source[0:1, 0:1], source[0:1, 0:1], ALU.mult).then_inc(turned, 1)


def experts(nc, ins, d, keep):
    with ExitStack() as ctx:
        sb = lambda n, s, dt=F32: ctx.enter_context(nc.sbuf_tensor(n, s, dt))
        ps = lambda n, s: ctx.enter_context(nc.psum_tensor(n, s, F32))
        sem = lambda n: ctx.enter_context(nc.semaphore(n))
        both = lambda n: [sem(f"{n}{b}") for b in range(2)]
        index = keep["index"]
        rows = keep["rows_raw"][0:HALF, :].rearrange("p (b h c) -> p b h c", b=2, h=2)
        gu_raw = keep["pair_raw"][:, :, :].rearrange("p b (c n) -> p b c n", c=NC)
        o_raw = keep["pair_raw"][:, :, :].rearrange("p b (h n) -> p b h n", h=HEADS)
        shared, x = (keep["rows_raw"][:, :].rearrange("p (a b c) -> p a b c", a=2, b=2)[:, a, :, :] for a in range(2))
        tick, dn_raw = sb("tick", [1, 1]), sb("dn_raw", [P, 2, NI, C])
        gu_hi, gu_lo = sb("gu_hi", [P, 2, NC, 2 * I], F32R), sb("gu_lo", [P, 2, NC, 2 * I], F32R)
        dn_hi, dn_lo = sb("dn_hi", [P, 2, NI, C], F32R), sb("dn_lo", [P, 2, NI, C], F32R)
        et_hi, et_lo = sb("et_hi", [P, 2, 2, 2 * CAP], F32R), sb("et_lo", [P, 2, 2, 2 * CAP], F32R)
        silu, inner = sb("silu", [P, 2, NI * CAP]), sb("inner", [P, 2, NI * CAP])
        in_hi, in_lo = sb("in_hi", [P, 2, NI, CAP], F32R), sb("in_lo", [P, 2, NI, CAP], F32R)
        rows_out = sb("rows_out", [HALF, 2, 2, C])
        wo_raw = sb("wo_raw", [P, 1, C])
        wo_hi, wo_lo = keep["wo_hi"], keep["wo_lo"]
        ident = keep["cst"][0:HALF, C_ID:C_ID + HALF]
        ones = keep["cst"][:, C_ONES:C_ONES + P]
        p_x, p_gu, p_y = ps("p_x", [P, 2, 512]), ps("p_gu", [P, 2, 2, 512]), ps("p_y", [P, 2, 512])

        index_loaded, gathered, gu_loaded, dn_loaded, stored = (
            both(n) for n in ("index_loaded", "gathered", "gu_loaded", "dn_loaded", "stored"))
        wo_loaded, wo_hi_ready, wo_ready = sem("wo_loaded"), sem("wo_hi_ready"), sem("wo_ready")
        gu_hi_ready, gu_ready = sem("gu_hi_ready"), sem("gu_ready")
        dn_hi_ready, dn_ready = sem("dn_hi_ready"), sem("dn_ready")
        x_psum, et_hi_ready, et_ready = sem("x_psum"), sem("et_hi_ready"), sem("et_ready")
        gu_done, silu_ready, inner_ready, in_hi_ready, in_ready = (
            sem(n) for n in ("gu_done", "esilu_ready", "inner_ready", "in_hi_ready", "in_ready"))
        y_done, y_evicted, turned = sem("y_done"), sem("y_evicted"), sem("turned")
        ahead_loaded = sem("ahead_loaded")
        block = ctx.enter_context(nc.Block())
        PAIRS = E // 2 - 2
        CR = 2

        @block.sync
        def _(sp):
            def load(e, b):
                sp.wait_ge(x_psum, e + 1)
                for h in range(2):
                    sp.dma_start(index[:, b, h:h + 1], d["slot_token"][bass.ds(e * CAP + h * HALF, HALF), :])\
                      .then_inc(index_loaded[b], 16)
                sp.wait_ge(gu_ready, e + 1)
                sp.dma_start(gu_raw[:, b, :, :], ins["wgu"][bass.ds(e, 1)].rearrange("e p c n -> p (e c) n")).then_inc(gu_loaded[b], 16)
                load_down(e, b)

            def load_down(e, b):
                sp.wait_ge(dn_ready, e + 1)
                sp.dma_start(dn_raw[:, b, :, :], ins["wdn"][bass.ds(e, 1)].rearrange("e p c n -> p (e c) n")).then_inc(dn_loaded[b], 16)
            for b in range(2):
                sp.sem_inc(gu_loaded[b], 16)
                sp.sem_inc(index_loaded[b], 32)
                load_down(b, b)
            sp.dma_start(wo_raw[:, :, :], ins["wo"][:, HEADS - 1:HEADS, :]).then_inc(wo_loaded, 16)
            with sp.Fori(0, E // 2 - 1) as i:
                for b in range(2):
                    load(2 * i + b + 2, b)
                sp.wait_ge(wo_ready, i + 1)
                sp.dma_start(wo_raw[:, :, :], ins["wo"][:, bass.ds(i, 1), :]).then_inc(wo_loaded, 16)
            for b in range(2):
                sp.wait_ge(gu_ready, E + b + 1)
                sp.dma_start(o_raw[:, b, :, :], d["o"].rearrange("h p n -> p h n")[:, :, b * P:(b + 1) * P]).then_inc(ahead_loaded, 16)
            sp.wait_ge(x_psum, E + CR)
            for b in range(2):
                sp.dma_start(shared[:, b, :], d["shared"][b * P:(b + 1) * P, :]).then_inc(ahead_loaded, 16)
                sp.dma_start(x[:, b, :], ins["x"][b * P:(b + 1) * P, :]).then_inc(ahead_loaded, 16)
            sp.wait_ge(ahead_loaded, 96)
            for b in range(2):
                sp.wait_ge(stored[b], 16 * (E // 2) + 16)

        @block.gpsimd
        def _(pool):
            def gather(e, b):
                pool.wait_ge(x_psum, e + 1)
                pool.wait_ge(index_loaded[b], 16 * (e - b) + 32)
                turn(nc, tick, ones, turned, e)
                for h in range(2):
                    pool.indirect_dma_start(rows[:, b, h, :], None, d["xn"],
                                            bass.IndirectOffsetOnAxis(ap=index[:, b, h:h + 1], axis=0),
                                            bounds_check=T - 1, oob_is_err=False).then_inc(gathered[b], 16)

            def split_down(e, b):
                pool.wait_ge(dn_loaded[b], 8 * (e - b) + 16)
                pool.wait_ge(y_done, e + 1)
                blocks = lambda m: m.rearrange("p a (u v) -> p (a u) v", v=P)
                nc.gpsimd.tensor_tensor(blocks(dn_hi[:, b, :, :]), blocks(dn_raw[:, b, :, :]),
                                        ones.unsqueeze(1).to_broadcast([P, NI * C // P, P]), ALU.mult).then_inc(dn_hi_ready, 1)
                pool.wait_ge(dn_hi_ready, e + 1)
                nc.gpsimd.tensor_tensor(dn_lo[:, b, :, :], dn_raw[:, b, :, :], dn_hi[:, b, :, :].bitcast(F32),
                                        ALU.subtract).then_inc(dn_ready, 1)
            pool.sem_inc(dn_ready, CR)
            pool.sem_inc(turned, 3)
            with pool.Fori(0, E // 2 - 1) as i:
                for b in range(2):
                    split_down(2 * i + b, b)
                    gather(2 * i + b + 2, b)
            split_down(E - 2, 0)
            split_down(E - 1, 1)



        @block.scalar
        def _(act):
            def weights(e, b):
                act.wait_ge(gu_loaded[b], 8 * (e - b) + 16)
                act.wait_ge(gu_done, e + 1)
                nc.scalar.activation(gu_hi[:, b, :, :], gu_raw[:, b, :, :], ACT.Copy).then_inc(gu_hi_ready, 1)

            def tokens(e, b):
                act.wait_ge(x_psum, e + 1 + CR)
                nc.scalar.activation(et_hi[:, b, :, :], p_x[:, :, 0:2 * CAP], ACT.Copy).then_inc(et_hi_ready, 1)

            def gate(e, b):
                act.wait_ge(gu_done, e + 1 + CR)
                nc.scalar.activation(silu[:, b, :], p_gu[:, b, 0, 0:NI * CAP], ACT.Silu).then_inc(silu_ready, 1)

            def evict(e, b):
                act.wait_ge(y_done, e + 1 + CR)
                act.wait_ge(stored[b], 8 * (e - b) + 16)
                nc.scalar.activation(rows_out[:, b, :, :], p_y[0:HALF, :, :], ACT.Copy).then_inc(y_evicted, 1)

            def store(e, b):
                act.wait_ge(y_evicted, e + 1 + 1)
                act.dma_start(d["expert"].rearrange("(e h p) c -> e p h c", h=2, p=HALF)[bass.ds(e, 1)]
                              .rearrange("e p h c -> p (e h) c"), rows_out[:, b, :, :]).then_inc(stored[b], 16)

            def project_weights(h, count):
                act.wait_ge(wo_loaded, 16 * count)
                nc.scalar.activation(wo_hi[:, bass.ds(h, 1), :], wo_raw[:, :, :], ACT.Copy).then_inc(wo_hi_ready, 1)
            for b in range(2):
                act.sem_inc(stored[b], 16)
            act.sem_inc(y_evicted, 1)
            def step(e, b, weights_ahead, tokens_ahead):
                gate(e, b)
                if tokens_ahead:
                    tokens(e + 1, 1 - b)
                if weights_ahead:
                    weights(e + 2, b)
                evict(e - 1, 1 - b)
                store(e - 1, 1 - b)
            weights(0, 0)
            tokens(0, 0)
            weights(1, 1)
            gate(0, 0)
            tokens(1, 1)
            weights(2, 0)
            project_weights(HEADS - 1, 1)
            with act.Fori(0, PAIRS) as i:
                step(2 * i + 1, 1, True, True)
                project_weights(i, i + 2)
                step(2 * i + 2, 0, True, True)
            step(E - 3, 1, True, True)
            project_weights(HEADS - 2, HEADS)
            step(E - 2, 0, False, True)
            step(E - 1, 1, False, False)
            evict(E - 1, 1)
            store(E - 1, 1)

        @block.vector
        def _(dve):
            v = nc.vector

            def weights(e, b):
                dve.wait_ge(gu_hi_ready, e + 1)
                v.tensor_tensor(gu_lo[:, b, :, :], gu_raw[:, b, :, :], gu_hi[:, b, :, :].bitcast(F32), ALU.subtract)\
                 .then_inc(gu_ready, 1)

            def tokens(e, b):
                dve.wait_ge(et_hi_ready, e + 1)
                v.tensor_tensor(et_lo[:, b, :, :], p_x[:, :, 0:2 * CAP], et_hi[:, b, :, :].bitcast(F32), ALU.subtract)\
                 .then_inc(et_ready, 1)

            def gate(e, b):
                dve.wait_ge(silu_ready, e + 1)
                v.tensor_tensor(inner[:, b, :], silu[:, b, :], p_gu[:, b, 1, 0:NI * CAP], ALU.mult).then_inc(inner_ready, 1)
                dve.wait_ge(inner_ready, e + 1)
                dve.wait_ge(y_done, e + 1)
                flat = lambda m: m[:, b, :, :].rearrange("p i n -> p (i n)")
                v.tensor_copy(flat(in_hi), inner[:, b, :]).then_inc(in_hi_ready, 1)
                dve.wait_ge(in_hi_ready, e + 1)
                v.tensor_tensor(flat(in_lo), inner[:, b, :], flat(in_hi).bitcast(F32), ALU.subtract).then_inc(in_ready, 1)

            def project_weights(h, count):
                dve.wait_ge(wo_hi_ready, count)
                v.tensor_tensor(wo_lo[:, bass.ds(h, 1), :], wo_raw[:, :, :],
                                wo_hi[:, bass.ds(h, 1), :].bitcast(F32), ALU.subtract).then_inc(wo_ready, 1)
            dve.sem_inc(gu_ready, CR)
            def step(e, b, weights_ahead, tokens_ahead):
                if tokens_ahead:
                    tokens(e + 1, 1 - b)
                gate(e, b)
                if weights_ahead:
                    weights(e + 2, b)
            weights(0, 0)
            tokens(0, 0)
            weights(1, 1)
            step(0, 0, True, True)
            project_weights(HEADS - 1, 1)
            with dve.Fori(0, PAIRS) as i:
                step(2 * i + 1, 1, True, True)
                project_weights(i, i + 2)
                step(2 * i + 2, 0, True, True)
            step(E - 3, 1, True, True)
            project_weights(HEADS - 2, HEADS)
            step(E - 2, 0, False, True)
            step(E - 1, 1, False, False)
            dve.wait_ge(wo_ready, HEADS)

        @block.tensor
        def _(pe):
            def tokens(e, b):
                if not (isinstance(e, int) and e < 2):
                    pe.wait_ge(gathered[b], 16 * (e - b))
                if not (isinstance(e, int) and e == 0):
                    pe.wait_ge(et_ready, e)
                for c in range(NC):
                    for h in range(2):
                        x = (c % 2) * CAP + h * HALF
                        last = nc.tensor.transpose(p_x[:, c // 2, x:x + HALF], rows[:, b, h, c * P:(c + 1) * P], ident)
                last.then_inc(x_psum, 1)

            def gate_up(e, b):
                pe.wait_ge(gu_ready, e + 1 + CR)
                pe.wait_ge(et_ready, e + 1)
                pe.wait_ge(in_ready, e + 1)
                for k in range(2 * NI):
                    x = (k % NI) * CAP
                    for c in range(NC):
                        w, t = slice(k * P, (k + 1) * P), slice((c % 2) * CAP, (c % 2 + 1) * CAP)
                        last = three_passes(nc, p_gu[:, b, k // NI, x:x + CAP], gu_hi[:, b, c, w], gu_lo[:, b, c, w],
                                            et_hi[:, b, c // 2, t], et_lo[:, b, c // 2, t], c == 0, c == NC - 1)
                last.then_inc(gu_done, 1)

            def down(e, b):
                pe.wait_ge(dn_ready, e + 1 + CR)
                pe.wait_ge(in_ready, e + 1 + CR)
                pe.wait_ge(y_evicted, e + 1)
                for h in range(2):
                    for i in range(NI):
                        a = slice(h * HALF, (h + 1) * HALF)
                        last = three_passes(nc, p_y[0:HALF, h, :], in_hi[:, b, i, a], in_lo[:, b, i, a],
                                            dn_hi[:, b, i, :], dn_lo[:, b, i, :], i == 0, i == NI - 1)
                last.then_inc(y_done, 1)
            pe.sem_inc(x_psum, CR)
            pe.sem_inc(gu_done, CR)
            pe.sem_inc(y_done, CR)
            pe.sem_inc(in_ready, CR)
            def step(e, b, tokens_ahead):
                gate_up(e, b)
                if tokens_ahead:
                    tokens(e + 1, 1 - b)
                down(e - 1, 1 - b)
            tokens(0, 0)
            gate_up(0, 0)
            tokens(1, 1)
            with pe.Fori(0, PAIRS) as i:
                step(2 * i + 1, 1, True)
                step(2 * i + 2, 0, True)
            step(E - 3, 1, True)
            step(E - 2, 0, True)
            step(E - 1, 1, False)
            down(E - 1, 1)


def combine(nc, ins, d, keep, out):
    with ExitStack() as ctx:
        sb = lambda n, s, dt=F32: ctx.enter_context(nc.sbuf_tensor(n, s, dt))
        sem = lambda n: ctx.enter_context(nc.semaphore(n))
        both = lambda n: [sem(f"{n}{b}") for b in range(2)]
        o_raw = keep["pair_raw"][:, :, :].rearrange("p b (h n) -> p b h n", h=HEADS)
        shared, x = (keep["rows_raw"][:, :].rearrange("p (a b c) -> p a b c", a=2, b=2)[:, a, :, :] for a in range(2))
        o_hi, o_lo = sb("o_hi", [P, 2, HEADS, P], F32R), sb("o_lo", [P, 2, HEADS, P], F32R)
        chosen = sb("chosen", [P, 2, K, C])
        mixed, gate, result = sb("mixed", [P, 2, C]), sb("gate", [P, 2, C]), sb("result", [P, 2, C])
        tick = sb("tick_c", [1, 1])
        slot, weight = sb("slot_now", [P, 2, K], U32), sb("weight_now", [P, 2, K])
        wo_hi, wo_lo = keep["wo_hi"], keep["wo_lo"]
        p_s = ctx.enter_context(nc.psum_tensor("p_proj", [P, 2, 512], F32))
        o_loaded, shared_loaded, x_loaded, chosen_loaded, written = (
            both(n) for n in ("o_loaded", "shared_row_loaded", "x_row_loaded", "chosen_loaded", "written"))
        weight_ready, slot_ready, turned = sem("weight_ready"), sem("slot_ready"), sem("turned_c")
        o_hi_ready, o_ready, s_done = sem("o_hi_ready"), sem("o_ready"), sem("s_done")
        mix_chain, gate_ready, end_chain, result_ready = sem("mix_chain"), sem("gate_ready"), sem("end_chain"), sem("result_ready")
        block = ctx.enter_context(nc.Block())
        CR = 2

        @block.sync
        def _(sp):
            def load_heads(t, b):
                sp.wait_ge(o_ready, t + 1)
                sp.dma_start(o_raw[:, b, :, :], d["o"].rearrange("h p n -> p h n")[:, :, bass.ds(t * P, P)]).then_inc(o_loaded[b], 16)

            def load_shared(t, b):
                sp.wait_ge(mix_chain, K * (t - 2) + 1)
                sp.dma_start(shared[:, b, :], d["shared"][bass.ds(t * P, P), :]).then_inc(shared_loaded[b], 16)

            def load_x(t, b):
                sp.wait_ge(result_ready, t + 1)
                sp.dma_start(x[:, b, :], ins["x"][bass.ds(t * P, P), :]).then_inc(x_loaded[b], 16)

            def store(t, b):
                sp.wait_ge(result_ready, t + 1 + CR)
                sp.dma_start(out[bass.ds(t * P, P), :], result[:, b, :]).then_inc(written[b], 16)
            for b in range(2):
                for loaded in (o_loaded, shared_loaded, x_loaded):
                    sp.sem_inc(loaded[b], 16)
            with sp.Fori(0, NT // 2 - 1) as i:
                for b in range(2):
                    load_heads(2 * i + b + 2, b)
                    load_shared(2 * i + b + 2, b)
                    store(2 * i + b, b)
                    load_x(2 * i + b + 2, b)
            for b in range(2):
                store(NT - 2 + b, b)
            for b in range(2):
                sp.wait_ge(written[b], 8 * NT + 16)

        @block.gpsimd
        def _(pool):
            pool.sem_inc(turned, 1)
            with pool.Fori(0, NT // 2) as i:
                for b in range(2):
                    pool.wait_ge(slot_ready, 2 * i + b + 1)
                    turn(nc, tick, keep["cst"], turned, 2 * i + b)
                    for k in range(K):
                        pool.indirect_dma_start(chosen[:, b, k, :], None, d["expert"],
                                                bass.IndirectOffsetOnAxis(ap=slot[:, b, k:k + 1], axis=0),
                                                bounds_check=E * CAP - 1, oob_is_err=False).then_inc(chosen_loaded[b], 16)

        @block.scalar
        def _(act):
            def tile(t, b):
                act.wait_ge(o_loaded[b], 8 * (t - b) + 16)
                act.wait_ge(s_done, t + 1)
                nc.scalar.activation(o_hi[:, b, :, :], o_raw[:, b, :, :], ACT.Copy).then_inc(o_hi_ready, 1)

            def gates(t, b):
                act.wait_ge(mix_chain, K * t + K)
                nc.scalar.activation(gate[:, b, :], mixed[:, b, :], ACT.Silu).then_inc(gate_ready, 1)
            for b in range(2):
                act.sem_inc(written[b], 16)
            with act.Fori(0, NT // 2) as i:
                for b in range(2):
                    tile(2 * i + b, b)
                    gates(2 * i + b, b)

        @block.vector
        def _(dve):
            v = nc.vector

            def tile(t, b, ahead):
                dve.wait_ge(o_hi_ready, t + 1)
                v.tensor_tensor(o_lo[:, b, :, :], o_raw[:, b, :, :], o_hi[:, b, :, :].bitcast(F32), ALU.subtract).then_inc(o_ready, 1)
                dve.wait_ge(shared_loaded[b], 8 * (t - b) + 16)
                dve.wait_ge(chosen_loaded[b], 8 * K * (t - b) + 16 * K)
                dve.wait_ge(weight_ready, t + 1)
                for k in range(K):
                    if k:
                        dve.wait_ge(mix_chain, K * t + k)
                    v.scalar_tensor_tensor(mixed[:, b, :], chosen[:, b, k, :], weight[:, b, k:k + 1],
                                           mixed[:, b, :] if k else shared[:, b, :], ALU.mult, ALU.add).then_inc(mix_chain, 1)
                if ahead:
                    next_slots(t + 2, b)

            def next_slots(t, b):
                if not (isinstance(t, int) and t < 2):
                    dve.wait_ge(mix_chain, K * (t - 1))
                v.tensor_copy(weight[:, b, :], keep["weight"][:, :, bass.ds(t, 1)].rearrange("p k t -> p (k t)")).then_inc(weight_ready, 1)
                v.tensor_copy(slot[:, b, :], keep["slot"][:, :, bass.ds(t, 1)].rearrange("p k t -> p (k t)")).then_inc(slot_ready, 1)

            def finish(t, b):
                dve.wait_ge(s_done, t + 1 + CR)
                dve.wait_ge(written[b], 8 * (t - b) + 16)
                dve.wait_ge(gate_ready, t + 1)
                v.tensor_tensor(result[:, b, :], p_s[:, b, :], gate[:, b, :], ALU.mult).then_inc(end_chain, 1)
                dve.wait_ge(x_loaded[b], 8 * (t - b) + 16)
                dve.wait_ge(end_chain, t + 1)
                v.tensor_tensor(result[:, b, :], result[:, b, :], x[:, b, :], ALU.add).then_inc(result_ready, 1)
            dve.sem_inc(o_ready, CR)
            dve.sem_inc(result_ready, CR)
            next_slots(0, 0)
            next_slots(1, 1)
            tile(0, 0, True)
            with dve.Fori(0, NT // 2 - 2) as i:
                tile(2 * i + 1, 1, True)
                finish(2 * i, 0)
                tile(2 * i + 2, 0, True)
                finish(2 * i + 1, 1)
            tile(NT - 3, 1, True)
            finish(NT - 4, 0)
            tile(NT - 2, 0, False)
            finish(NT - 3, 1)
            tile(NT - 1, 1, False)
            finish(NT - 2, 0)
            finish(NT - 1, 1)

        @block.tensor
        def _(pe):
            pe.sem_inc(s_done, CR)
            with pe.Fori(0, NT // 2) as i:
                for b in range(2):
                    t = 2 * i + b
                    pe.wait_ge(o_ready, t + 1 + CR)
                    pe.wait_ge(result_ready, t + 1)
                    nc.tensor.matmul(p_s[:, b, :], keep["one_r"][:, :], keep["bo_hi"][:, :], start=True, stop=False)
                    nc.tensor.matmul(p_s[:, b, :], keep["one_r"][:, :], keep["bo_lo"][:, :], start=False, stop=False)
                    for h in range(HEADS):
                        last = three_passes(nc, p_s[:, b, :], o_hi[:, b, h, :], o_lo[:, b, h, :],
                                            wo_hi[:, h, :], wo_lo[:, h, :], False, h == HEADS - 1)
                    last.then_inc(s_done, 1)


def build(nc, ins, out):
    d = {
        "xn": nc.dram_tensor("xn_rows", (T, C), F32).ap(),
        "qk": nc.dram_tensor("qk_heads", (ROPED, P, T), F32).ap(),
        "v": nc.dram_tensor("v_rows", (T, KV * HD), F32).ap(),
        "o": nc.dram_tensor("o_heads", (HEADS, P, T), F32).ap(),
        "inv": nc.dram_tensor("inverse_sums", (KV * G * NG, TG), F32).ap(),
        "slot_token": nc.dram_tensor("slot_token", (E * CAP, 1), U32).ap(),
        "expert": nc.dram_tensor("expert_rows", (E * CAP, C), F32).ap(),
        "shared": nc.dram_tensor("shared_rows", (T, C), F32).ap(),
    }
    with ExitStack() as ctx:
        sb = lambda n, s, dt=F32: ctx.enter_context(nc.sbuf_tensor(n, s, dt))
        keep = {"cst": sb("cst", [P, C_END]), "slot": sb("slot", [P, K, NT], U32), "weight": sb("weight", [P, K, NT])}
        keep |= {n: sb(n, [1, w], F32R) for n, w in (("one_r", P), ("bo_hi", C), ("bo_lo", C))}
        project(nc, ins, d, keep)
        nc.disable_value_cache = True
        keep |= {"pair_raw": sb("pair_raw", [P, 2, NG * TG]), "rows_raw": sb("rows_raw", [P, NT * HD]),
                 "index": sb("index", [HALF, 2, 2], U32)}
        attend(nc, ins, d, keep)
        keep["wo_hi"], keep["wo_lo"] = sb("wo_hi", [P, HEADS, C], F32R), sb("wo_lo", [P, HEADS, C], F32R)
        experts(nc, ins, d, keep)
        combine(nc, ins, d, keep, out)


def lay_out(L0_attn_x, L0_attn_Wq, L0_attn_bq, L0_attn_Wk, L0_attn_bk, L0_attn_Wv, L0_attn_bv, L0_attn_Wo,
            L0_attn_bo, L0_ffn_gate_w, L0_ffn_bias, L0_ffn_w_gate, L0_ffn_w_up, L0_ffn_w_down, L0_ffn_sg,
            L0_ffn_su, L0_ffn_sd):
    a = np.ascontiguousarray
    split = np.concatenate([np.arange(0, HD, 2), np.arange(1, HD, 2)])
    wq = np.asarray(L0_attn_Wq).reshape(C, G, KV, HD).transpose(2, 1, 0, 3).reshape(HEADS, C, HD)
    wk = np.asarray(L0_attn_Wk).reshape(C, KV, HD).transpose(1, 0, 2)
    w = np.concatenate([wq, wk])[:, :, split]
    bq = np.asarray(L0_attn_bq).reshape(G, KV, HD).transpose(1, 0, 2).reshape(HEADS, HD)
    b = np.concatenate([bq, np.asarray(L0_attn_bk).reshape(KV, HD)])[:, split]
    wqk = np.concatenate([w.reshape(ROPED, NC, P, HD).transpose(0, 2, 1, 3).reshape(ROPED, P, NC * HD),
                          b[:, :, None]], axis=2)

    def rows(m):
        m = np.swapaxes(np.asarray(m), -1, -2)
        m = m.reshape(*m.shape[:-2], m.shape[-2] // P, P, m.shape[-1])
        return np.swapaxes(m, -3, -2)
    return {
        "x": a(np.asarray(L0_attn_x).reshape(T, C)),
        "wqk": a(wqk),
        "wv": a(rows(np.asarray(L0_attn_Wv).T)),
        "bv": a(np.asarray(L0_attn_bv).reshape(1, -1)),
        "wo": a(rows(np.asarray(L0_attn_Wo).T)),
        "bo": a(np.asarray(L0_attn_bo).reshape(1, -1)),
        "gate_w": a(rows(L0_ffn_gate_w)),
        "ebias": a(np.asarray(L0_ffn_bias)),
        "wgu": a(np.concatenate([rows(L0_ffn_w_gate), rows(L0_ffn_w_up)], axis=3)),
        "wdn": a(rows(L0_ffn_w_down)),
        "sgu": a(np.concatenate([rows(L0_ffn_sg), rows(L0_ffn_su)], axis=2)),
        "sdn": a(rows(L0_ffn_sd)),
        "cst": constant_table(),
        "rope": rope_table(),
        "tok": (np.arange(NT, dtype=np.uint32)[None, :] * P + np.arange(P, dtype=np.uint32)[:, None]).astype(np.uint32),
    }


def kernel(**inputs):
    import concourse.bacc as bacc
    from concourse.bass_utils import run_bass_kernel_spmd

    nc = bacc.Bacc("TRN2", target_bir_lowering=False, num_devices=1)
    arrays = lay_out(**inputs)
    ins = {n: nc.dram_tensor(f"in_{n}", v.shape, mybir.dt.from_np(v.dtype), kind="ExternalInput").ap()
           for n, v in arrays.items()}
    out = nc.dram_tensor("out", (T, C), F32, kind="ExternalOutput").ap()
    build(nc, ins, out)
    r = run_bass_kernel_spmd(nc, [{f"in_{n}": v for n, v in arrays.items()}], core_ids=[0])
    return r.results[0]["out"].reshape(1, T, C)
```
